# Optimizing a Trainium2 kernel written in Bass

```python
import numpy as np
import jax
import jax.numpy as jnp

def _softmax(x, axis=-1):
    return jax.nn.softmax(x, axis=axis)
def _gelu(x):
    return jax.nn.gelu(x, approximate=True)
def _silu(x):
    return jax.nn.silu(x)
def _sigmoid(x):
    return jax.nn.sigmoid(x)
def _layernorm(x, axis=-1, eps=1e-5):
    m = jnp.mean(x, axis=axis, keepdims=True)
    v = jnp.var(x, axis=axis, keepdims=True)
    return (x - m) / jnp.sqrt(v + eps)
def _scatter_add(tgt, idx, src, axis=0):
    return tgt.at[idx].add(src)
def _segment_sum(src, seg, n):
    return jax.ops.segment_sum(src, seg, n)

kernel_name = 'mk_conv_seq_d4_conv_nhwc256_eb7967'

def setup_inputs(seed: int = 0):
    np.random.seed(seed)
    _w = jnp.asarray
    def _rec_inputs():
        import jax
        import jax.numpy as jnp
        _gk = jax.random.key(seed)
        x = -0.0005153 + 1.001 * jax.random.normal(jax.random.fold_in(_gk, 1), (4, 56, 56, 256), jnp.float32)
        return x
    x = _rec_inputs()
    def _L0_conv_setup():
        import jax, jax.numpy as jnp
        import numpy as np
        B, H, W, C, G = (4, 56, 56, 256, 16)
        K = 9
        GC = C // G

        def _ln(x, g, b, eps=1e-05):
            mu = jnp.mean(x, axis=-1, keepdims=True)
            var = jnp.mean(jnp.square(x - mu), axis=-1, keepdims=True)
            return (x - mu) * jax.lax.rsqrt(var + eps) * g + b

        def _gelu(x):
            return jax.nn.gelu(x, approximate=False)

        def _dcnv3_core(x, offset, mask):
            xg = x.reshape(B, H * W, G, GC)
            off = offset.reshape(B, H, W, G, K, 2)
            dy, dx = jnp.meshgrid(jnp.arange(-1.0, 2.0), jnp.arange(-1.0, 2.0), indexing='ij')
            dx = dx.reshape(K).astype(x.dtype)
            dy = dy.reshape(K).astype(x.dtype)
            gx = jnp.arange(W, dtype=x.dtype)[None, None, :, None, None]
            gy = jnp.arange(H, dtype=x.dtype)[None, :, None, None, None]
            px = gx + dx + off[..., 0]
            py = gy + dy + off[..., 1]

            def flat(p):
                return p.transpose(0, 1, 2, 4, 3).reshape(B, H * W * K, G)
            pxf, pyf = (flat(px), flat(py))
            x0 = jnp.floor(pxf)
            y0 = jnp.floor(pyf)
            acc = jnp.zeros((B, H * W * K, G, GC), x.dtype)
            for cx, cy in ((x0, y0), (x0 + 1, y0), (x0, y0 + 1), (x0 + 1, y0 + 1)):
                wgt = (1 - jnp.abs(pxf - cx)) * (1 - jnp.abs(pyf - cy))
                valid = ((cx >= 0) & (cx < W) & (cy >= 0) & (cy < H)).astype(x.dtype)
                idx = (jnp.clip(cy, 0, H - 1).astype(jnp.int32) * W + jnp.clip(cx, 0, W - 1).astype(jnp.int32))[..., None]
                v = jnp.take_along_axis(xg, idx, axis=1)
                acc = acc + (wgt * valid)[..., None] * v
            mf = flat(mask)[..., None]
            out = (acc * mf).reshape(B, H * W, K, G, GC).sum(axis=2)
            return out.reshape(B, H, W, C)

        def _dcn(x, w_in, b_in, w_dw, b_dw, ln_dw_g, ln_dw_b, w_off, b_off, w_mask, b_mask, w_out, b_out):
            xp = x @ w_in + b_in
            x1 = jax.lax.conv_general_dilated(x, w_dw, window_strides=(1, 1), padding='SAME', dimension_numbers=('NHWC', 'HWIO', 'NHWC'), feature_group_count=C) + b_dw
            x1 = _gelu(_ln(x1, ln_dw_g, ln_dw_b))
            offset = x1 @ w_off + b_off
            mask = jax.nn.softmax((x1 @ w_mask + b_mask).reshape(B, H, W, G, K), axis=-1)
            y = _dcnv3_core(xp, offset, mask)
            return y @ w_out + b_out

        def _block(x, w_in, b_in, w_dw, b_dw, ln_dw_g, ln_dw_b, w_off, b_off, w_mask, b_mask, w_out, b_out, ln1_g, ln1_b, w_fc1, b_fc1, w_fc2, b_fc2, ln2_g, ln2_b, gamma1, gamma2):
            y = _dcn(x, w_in, b_in, w_dw, b_dw, ln_dw_g, ln_dw_b, w_off, b_off, w_mask, b_mask, w_out, b_out)
            x = x + gamma1 * _ln(y, ln1_g, ln1_b)
            m = _gelu(x @ w_fc1 + b_fc1) @ w_fc2 + b_fc2
            x = x + gamma2 * _ln(m, ln2_g, ln2_b)
            return x
        key = jax.random.key(seed)
        ks = jax.random.split(key, 9)
        f = jnp.float32

        def rn(k, shape, s=0.02):
            return jax.random.normal(k, shape, dtype=f) * s
        return {'x': jax.random.normal(ks[0], (B, H, W, C), dtype=f), 'w_in': rn(ks[1], (C, C)), 'b_in': jnp.zeros((C,), f), 'w_dw': rn(ks[2], (3, 3, 1, C), 0.1), 'b_dw': jnp.zeros((C,), f), 'ln_dw_g': jnp.ones((C,), f), 'ln_dw_b': jnp.zeros((C,), f), 'w_off': rn(ks[3], (C, G * K * 2)), 'b_off': jnp.zeros((G * K * 2,), f), 'w_mask': rn(ks[4], (C, G * K)), 'b_mask': jnp.zeros((G * K,), f), 'w_out': rn(ks[5], (C, C)), 'b_out': jnp.zeros((C,), f), 'ln1_g': jnp.ones((C,), f), 'ln1_b': jnp.zeros((C,), f), 'w_fc1': rn(ks[6], (C, C)), 'b_fc1': jnp.zeros((C,), f), 'w_fc2': rn(ks[7], (C, C)), 'b_fc2': jnp.zeros((C,), f), 'ln2_g': jnp.ones((C,), f), 'ln2_b': jnp.zeros((C,), f), 'gamma1': jnp.ones((C,), f), 'gamma2': jnp.ones((C,), f)}
    _L0_conv_all = _L0_conv_setup()
    _L0_conv_in = {k: v for k, v in _L0_conv_all.items() if k in ('w_in', 'b_in', 'w_dw', 'b_dw', 'ln_dw_g', 'ln_dw_b', 'w_off', 'b_off', 'w_mask', 'b_mask', 'w_out', 'b_out', 'ln1_g', 'ln1_b', 'w_fc1', 'b_fc1', 'w_fc2', 'b_fc2', 'ln2_g', 'ln2_b', 'gamma1', 'gamma2', )}
    del _L0_conv_all

    def _L1_conv_setup():
        import jax, jax.numpy as jnp
        import numpy as np
        B, H, W, C = (32, 56, 56, 256)
        NH, WS, SH = (8, 7, 3)
        HD = C // NH
        SCALE = HD ** (-0.5)
        N = WS * WS
        MLP = 4 * C

        def _rel_pos_index():
            coords = np.stack(np.meshgrid(np.arange(WS), np.arange(WS), indexing='ij')).reshape(2, -1)
            rel = (coords[:, :, None] - coords[:, None, :]).transpose(1, 2, 0)
            rel[..., 0] += WS - 1
            rel[..., 1] += WS - 1
            rel[..., 0] *= 2 * WS - 1
            return jnp.asarray(rel.sum(-1))

        def _attn_mask():
            img = np.zeros((H, W))
            cnt = 0
            for hs in (slice(0, -WS), slice(-WS, -SH), slice(-SH, None)):
                for ws_ in (slice(0, -WS), slice(-WS, -SH), slice(-SH, None)):
                    img[hs, ws_] = cnt
                    cnt += 1
            mw = img.reshape(H // WS, WS, W // WS, WS).transpose(0, 2, 1, 3).reshape(-1, N)
            am = mw[:, None, :] - mw[:, :, None]
            am = np.where(am != 0, -1000000000.0, 0.0).astype(np.float32)
            return jnp.asarray(am)

        def _part(x):
            b = x.shape[0]
            x = x.reshape(b, H // WS, WS, W // WS, WS, C)
            return x.transpose(0, 1, 3, 2, 4, 5).reshape(-1, N, C)

        def _rev(xw):
            x = xw.reshape(-1, H // WS, W // WS, WS, WS, C)
            return x.transpose(0, 1, 3, 2, 4, 5).reshape(-1, H, W, C)

        def _ln(x, g, b):
            m = x.mean(-1, keepdims=True)
            v = x.var(-1, keepdims=True)
            return (x - m) / jnp.sqrt(v + 1e-05) * g + b
        key = jax.random.key(seed)
        ks = jax.random.split(key, 6)
        s = 0.02
        return {'x': jax.random.normal(ks[0], (B, H, W, C), jnp.float32), 'gamma1': jnp.ones((C,), jnp.float32), 'beta1': jnp.zeros((C,), jnp.float32), 'w_qkv': jax.random.normal(ks[1], (C, 3 * C), jnp.float32) * s, 'b_qkv': jnp.zeros((3 * C,), jnp.float32), 'rpb': jax.random.normal(ks[2], ((2 * WS - 1) ** 2, NH), jnp.float32) * s, 'w_proj': jax.random.normal(ks[3], (C, C), jnp.float32) * s, 'b_proj': jnp.zeros((C,), jnp.float32), 'gamma2': jnp.ones((C,), jnp.float32), 'beta2': jnp.zeros((C,), jnp.float32), 'w_fc1': jax.random.normal(ks[4], (C, MLP), jnp.float32) * s, 'b_fc1': jnp.zeros((MLP,), jnp.float32), 'w_fc2': jax.random.normal(ks[5], (MLP, C), jnp.float32) * s, 'b_fc2': jnp.zeros((C,), jnp.float32)}
    _L1_conv_all = _L1_conv_setup()
    _L1_conv_in = {k: v for k, v in _L1_conv_all.items() if k in ('gamma1', 'beta1', 'w_qkv', 'b_qkv', 'rpb', 'w_proj', 'b_proj', 'gamma2', 'beta2', 'w_fc1', 'b_fc1', 'w_fc2', 'b_fc2', )}
    del _L1_conv_all

    def _L2_conv_setup():
        import jax, jax.numpy as jnp
        import numpy as np
        NUM_BLOCKS = 8
        HSF = 1
        LAMBDA = 0.01
        HTF = 1.0
        SCALE = 0.02

        def softshrink(v, lam):
            return jnp.where(v > lam, v - lam, jnp.where(v < -lam, v + lam, jnp.zeros_like(v)))
        key = jax.random.key(seed)
        ks = jax.random.split(key, 5)
        B, H, W, C = (1, 360, 720, 256)
        bs = C // NUM_BLOCKS
        x = jax.random.normal(ks[0], (B, H, W, C), dtype=jnp.float32)
        w1 = SCALE * jax.random.normal(ks[1], (2, NUM_BLOCKS, bs, bs * HSF), dtype=jnp.float32)
        b1 = SCALE * jax.random.normal(ks[2], (2, NUM_BLOCKS, bs * HSF), dtype=jnp.float32)
        w2 = SCALE * jax.random.normal(ks[3], (2, NUM_BLOCKS, bs * HSF, bs), dtype=jnp.float32)
        b2 = SCALE * jax.random.normal(ks[4], (2, NUM_BLOCKS, bs), dtype=jnp.float32)
        return {'x': x, 'w1': w1, 'b1': b1, 'w2': w2, 'b2': b2}
    _L2_conv_all = _L2_conv_setup()
    _L2_conv_in = {k: v for k, v in _L2_conv_all.items() if k in ('w1', 'b1', 'w2', 'b2', )}
    del _L2_conv_all

    def _L3_conv_setup():
        import jax, jax.numpy as jnp
        import numpy as np
        DIM = 256
        HEADS = 8
        WS = 8
        N = WS * WS
        NF = 2 * (N // 2 + 1)
        HD = DIM // HEADS
        SCALE = HD ** (-0.5)
        EPS = 1e-05

        def _rel_pos_index():
            ch = np.arange(WS)
            coords = np.stack(np.meshgrid(ch, ch, indexing='ij'))
            cf = coords.reshape(2, -1)
            rel = cf[:, :, None] - cf[:, None, :]
            rel = rel.transpose(1, 2, 0).astype(np.int64)
            rel[..., 0] += WS - 1
            rel[..., 1] += WS - 1
            rel[..., 0] *= 2 * WS - 1
            return jnp.asarray(rel.sum(-1))
        REL_IDX = _rel_pos_index()

        def _ln(x, w, b):
            m = jnp.mean(x, -1, keepdims=True)
            v = jnp.mean((x - m) ** 2, -1, keepdims=True)
            return (x - m) * jax.lax.rsqrt(v + EPS) * w + b

        def _attn_scores(t, qkv_w, qkv_b):
            Bw, Nt, C = t.shape
            qkv = (t @ qkv_w.T + qkv_b).reshape(Bw, Nt, 3, HEADS, HD)
            q, k, v = jnp.moveaxis(qkv, 2, 0)
            q = q.transpose(0, 2, 1, 3)
            k = k.transpose(0, 2, 1, 3)
            v = v.transpose(0, 2, 1, 3)
            a = jnp.einsum('bhnd,bhmd->bhnm', q, k) * SCALE
            return (a, v)
        key = jax.random.key(seed)
        ks = jax.random.split(key, 16)
        B, H, W, C = (2, 256, 256, DIM)
        p = 0.02
        return {'x': jax.random.normal(ks[0], (B, H, W, C), jnp.float32), 'mask_matrix': jnp.zeros((H // WS * (W // WS), N, N), jnp.float32), 'norm1_w': jnp.ones((C,), jnp.float32), 'norm1_b': jnp.zeros((C,), jnp.float32), 'qkv_w': jax.random.normal(ks[1], (3 * C, C), jnp.float32) * p, 'qkv_b': jnp.zeros((3 * C,), jnp.float32), 'rpb_table': jax.random.normal(ks[2], ((2 * WS - 1) ** 2, HEADS), jnp.float32) * p, 'proj_w': jax.random.normal(ks[3], (C, C), jnp.float32) * p, 'proj_b': jnp.zeros((C,), jnp.float32), 'norm2_w': jnp.ones((C,), jnp.float32), 'norm2_b': jnp.zeros((C,), jnp.float32), 'fc1_w': jax.random.normal(ks[4], (4 * C, C), jnp.float32) * p, 'fc1_b': jnp.zeros((4 * C,), jnp.float32), 'fc2_w': jax.random.normal(ks[5], (C, 4 * C), jnp.float32) * p, 'fc2_b': jnp.zeros((C,), jnp.float32)}
    _L3_conv_all = _L3_conv_setup()
    _L3_conv_in = {k: v for k, v in _L3_conv_all.items() if k in ('mask_matrix', 'norm1_w', 'norm1_b', 'qkv_w', 'qkv_b', 'rpb_table', 'proj_w', 'proj_b', 'norm2_w', 'norm2_b', 'fc1_w', 'fc1_b', 'fc2_w', 'fc2_b', )}
    del _L3_conv_all

    return {
        "x": x,
        "L0_conv_w_in": _L0_conv_in["w_in"],
        "L0_conv_b_in": _L0_conv_in["b_in"],
        "L0_conv_w_dw": _L0_conv_in["w_dw"],
        "L0_conv_b_dw": _L0_conv_in["b_dw"],
        "L0_conv_ln_dw_g": _L0_conv_in["ln_dw_g"],
        "L0_conv_ln_dw_b": _L0_conv_in["ln_dw_b"],
        "L0_conv_w_off": _L0_conv_in["w_off"],
        "L0_conv_b_off": _L0_conv_in["b_off"],
        "L0_conv_w_mask": _L0_conv_in["w_mask"],
        "L0_conv_b_mask": _L0_conv_in["b_mask"],
        "L0_conv_w_out": _L0_conv_in["w_out"],
        "L0_conv_b_out": _L0_conv_in["b_out"],
        "L0_conv_ln1_g": _L0_conv_in["ln1_g"],
        "L0_conv_ln1_b": _L0_conv_in["ln1_b"],
        "L0_conv_w_fc1": _L0_conv_in["w_fc1"],
        "L0_conv_b_fc1": _L0_conv_in["b_fc1"],
        "L0_conv_w_fc2": _L0_conv_in["w_fc2"],
        "L0_conv_b_fc2": _L0_conv_in["b_fc2"],
        "L0_conv_ln2_g": _L0_conv_in["ln2_g"],
        "L0_conv_ln2_b": _L0_conv_in["ln2_b"],
        "L0_conv_gamma1": _L0_conv_in["gamma1"],
        "L0_conv_gamma2": _L0_conv_in["gamma2"],
        "L1_conv_gamma1": _L1_conv_in["gamma1"],
        "L1_conv_beta1": _L1_conv_in["beta1"],
        "L1_conv_w_qkv": _L1_conv_in["w_qkv"],
        "L1_conv_b_qkv": _L1_conv_in["b_qkv"],
        "L1_conv_rpb": _L1_conv_in["rpb"],
        "L1_conv_w_proj": _L1_conv_in["w_proj"],
        "L1_conv_b_proj": _L1_conv_in["b_proj"],
        "L1_conv_gamma2": _L1_conv_in["gamma2"],
        "L1_conv_beta2": _L1_conv_in["beta2"],
        "L1_conv_w_fc1": _L1_conv_in["w_fc1"],
        "L1_conv_b_fc1": _L1_conv_in["b_fc1"],
        "L1_conv_w_fc2": _L1_conv_in["w_fc2"],
        "L1_conv_b_fc2": _L1_conv_in["b_fc2"],
        "L2_conv_w1": _L2_conv_in["w1"],
        "L2_conv_b1": _L2_conv_in["b1"],
        "L2_conv_w2": _L2_conv_in["w2"],
        "L2_conv_b2": _L2_conv_in["b2"],
        "L3_conv_mask_matrix": _L3_conv_in["mask_matrix"],
        "L3_conv_norm1_w": _L3_conv_in["norm1_w"],
        "L3_conv_norm1_b": _L3_conv_in["norm1_b"],
        "L3_conv_qkv_w": _L3_conv_in["qkv_w"],
        "L3_conv_qkv_b": _L3_conv_in["qkv_b"],
        "L3_conv_rpb_table": _L3_conv_in["rpb_table"],
        "L3_conv_proj_w": _L3_conv_in["proj_w"],
        "L3_conv_proj_b": _L3_conv_in["proj_b"],
        "L3_conv_norm2_w": _L3_conv_in["norm2_w"],
        "L3_conv_norm2_b": _L3_conv_in["norm2_b"],
        "L3_conv_fc1_w": _L3_conv_in["fc1_w"],
        "L3_conv_fc1_b": _L3_conv_in["fc1_b"],
        "L3_conv_fc2_w": _L3_conv_in["fc2_w"],
        "L3_conv_fc2_b": _L3_conv_in["fc2_b"],
    }

def reference(x, L0_conv_w_in, L0_conv_b_in, L0_conv_w_dw, L0_conv_b_dw, L0_conv_ln_dw_g, L0_conv_ln_dw_b, L0_conv_w_off, L0_conv_b_off, L0_conv_w_mask, L0_conv_b_mask, L0_conv_w_out, L0_conv_b_out, L0_conv_ln1_g, L0_conv_ln1_b, L0_conv_w_fc1, L0_conv_b_fc1, L0_conv_w_fc2, L0_conv_b_fc2, L0_conv_ln2_g, L0_conv_ln2_b, L0_conv_gamma1, L0_conv_gamma2, L1_conv_gamma1, L1_conv_beta1, L1_conv_w_qkv, L1_conv_b_qkv, L1_conv_rpb, L1_conv_w_proj, L1_conv_b_proj, L1_conv_gamma2, L1_conv_beta2, L1_conv_w_fc1, L1_conv_b_fc1, L1_conv_w_fc2, L1_conv_b_fc2, L2_conv_w1, L2_conv_b1, L2_conv_w2, L2_conv_b2, L3_conv_mask_matrix, L3_conv_norm1_w, L3_conv_norm1_b, L3_conv_qkv_w, L3_conv_qkv_b, L3_conv_rpb_table, L3_conv_proj_w, L3_conv_proj_b, L3_conv_norm2_w, L3_conv_norm2_b, L3_conv_fc1_w, L3_conv_fc1_b, L3_conv_fc2_w, L3_conv_fc2_b):
    import jax
    import jax.numpy as jnp
    def _L0_conv_ref(x, w_in, b_in, w_dw, b_dw, ln_dw_g, ln_dw_b, w_off, b_off, w_mask, b_mask, w_out, b_out, ln1_g, ln1_b, w_fc1, b_fc1, w_fc2, b_fc2, ln2_g, ln2_b, gamma1, gamma2):
        import jax, jax.numpy as jnp
        import numpy as np
        B, H, W, C, G = (4, 56, 56, 256, 16)
        K = 9
        GC = C // G

        def _ln(x, g, b, eps=1e-05):
            mu = jnp.mean(x, axis=-1, keepdims=True)
            var = jnp.mean(jnp.square(x - mu), axis=-1, keepdims=True)
            return (x - mu) * jax.lax.rsqrt(var + eps) * g + b

        def _gelu(x):
            return jax.nn.gelu(x, approximate=False)

        def _dcnv3_core(x, offset, mask):
            xg = x.reshape(B, H * W, G, GC)
            off = offset.reshape(B, H, W, G, K, 2)
            dy, dx = jnp.meshgrid(jnp.arange(-1.0, 2.0), jnp.arange(-1.0, 2.0), indexing='ij')
            dx = dx.reshape(K).astype(x.dtype)
            dy = dy.reshape(K).astype(x.dtype)
            gx = jnp.arange(W, dtype=x.dtype)[None, None, :, None, None]
            gy = jnp.arange(H, dtype=x.dtype)[None, :, None, None, None]
            px = gx + dx + off[..., 0]
            py = gy + dy + off[..., 1]

            def flat(p):
                return p.transpose(0, 1, 2, 4, 3).reshape(B, H * W * K, G)
            pxf, pyf = (flat(px), flat(py))
            x0 = jnp.floor(pxf)
            y0 = jnp.floor(pyf)
            acc = jnp.zeros((B, H * W * K, G, GC), x.dtype)
            for cx, cy in ((x0, y0), (x0 + 1, y0), (x0, y0 + 1), (x0 + 1, y0 + 1)):
                wgt = (1 - jnp.abs(pxf - cx)) * (1 - jnp.abs(pyf - cy))
                valid = ((cx >= 0) & (cx < W) & (cy >= 0) & (cy < H)).astype(x.dtype)
                idx = (jnp.clip(cy, 0, H - 1).astype(jnp.int32) * W + jnp.clip(cx, 0, W - 1).astype(jnp.int32))[..., None]
                v = jnp.take_along_axis(xg, idx, axis=1)
                acc = acc + (wgt * valid)[..., None] * v
            mf = flat(mask)[..., None]
            out = (acc * mf).reshape(B, H * W, K, G, GC).sum(axis=2)
            return out.reshape(B, H, W, C)

        def _dcn(x, w_in, b_in, w_dw, b_dw, ln_dw_g, ln_dw_b, w_off, b_off, w_mask, b_mask, w_out, b_out):
            xp = x @ w_in + b_in
            x1 = jax.lax.conv_general_dilated(x, w_dw, window_strides=(1, 1), padding='SAME', dimension_numbers=('NHWC', 'HWIO', 'NHWC'), feature_group_count=C) + b_dw
            x1 = _gelu(_ln(x1, ln_dw_g, ln_dw_b))
            offset = x1 @ w_off + b_off
            mask = jax.nn.softmax((x1 @ w_mask + b_mask).reshape(B, H, W, G, K), axis=-1)
            y = _dcnv3_core(xp, offset, mask)
            return y @ w_out + b_out

        def _block(x, w_in, b_in, w_dw, b_dw, ln_dw_g, ln_dw_b, w_off, b_off, w_mask, b_mask, w_out, b_out, ln1_g, ln1_b, w_fc1, b_fc1, w_fc2, b_fc2, ln2_g, ln2_b, gamma1, gamma2):
            y = _dcn(x, w_in, b_in, w_dw, b_dw, ln_dw_g, ln_dw_b, w_off, b_off, w_mask, b_mask, w_out, b_out)
            x = x + gamma1 * _ln(y, ln1_g, ln1_b)
            m = _gelu(x @ w_fc1 + b_fc1) @ w_fc2 + b_fc2
            x = x + gamma2 * _ln(m, ln2_g, ln2_b)
            return x
        return _block(x, w_in, b_in, w_dw, b_dw, ln_dw_g, ln_dw_b, w_off, b_off, w_mask, b_mask, w_out, b_out, ln1_g, ln1_b, w_fc1, b_fc1, w_fc2, b_fc2, ln2_g, ln2_b, gamma1, gamma2)

    def _L1_conv_ref(x, gamma1, beta1, w_qkv, b_qkv, rpb, w_proj, b_proj, gamma2, beta2, w_fc1, b_fc1, w_fc2, b_fc2):
        import jax, jax.numpy as jnp
        import numpy as np
        B, H, W, C = (32, 56, 56, 256)
        NH, WS, SH = (8, 7, 3)
        HD = C // NH
        SCALE = HD ** (-0.5)
        N = WS * WS
        MLP = 4 * C

        def _rel_pos_index():
            coords = np.stack(np.meshgrid(np.arange(WS), np.arange(WS), indexing='ij')).reshape(2, -1)
            rel = (coords[:, :, None] - coords[:, None, :]).transpose(1, 2, 0)
            rel[..., 0] += WS - 1
            rel[..., 1] += WS - 1
            rel[..., 0] *= 2 * WS - 1
            return jnp.asarray(rel.sum(-1))

        def _attn_mask():
            img = np.zeros((H, W))
            cnt = 0
            for hs in (slice(0, -WS), slice(-WS, -SH), slice(-SH, None)):
                for ws_ in (slice(0, -WS), slice(-WS, -SH), slice(-SH, None)):
                    img[hs, ws_] = cnt
                    cnt += 1
            mw = img.reshape(H // WS, WS, W // WS, WS).transpose(0, 2, 1, 3).reshape(-1, N)
            am = mw[:, None, :] - mw[:, :, None]
            am = np.where(am != 0, -1000000000.0, 0.0).astype(np.float32)
            return jnp.asarray(am)

        def _part(x):
            b = x.shape[0]
            x = x.reshape(b, H // WS, WS, W // WS, WS, C)
            return x.transpose(0, 1, 3, 2, 4, 5).reshape(-1, N, C)

        def _rev(xw):
            x = xw.reshape(-1, H // WS, W // WS, WS, WS, C)
            return x.transpose(0, 1, 3, 2, 4, 5).reshape(-1, H, W, C)

        def _ln(x, g, b):
            m = x.mean(-1, keepdims=True)
            v = x.var(-1, keepdims=True)
            return (x - m) / jnp.sqrt(v + 1e-05) * g + b
        idx = _rel_pos_index()
        mask = _attn_mask()
        nW = mask.shape[0]
        shortcut = x
        xn = _ln(x, gamma1, beta1)
        xs = jnp.roll(xn, (-SH, -SH), axis=(1, 2))
        xw = _part(xs)
        qkv = (xw @ w_qkv + b_qkv).reshape(-1, N, 3, NH, HD).transpose(2, 0, 3, 1, 4)
        q, k, v = (jax.nn.relu(qkv[0]), jax.nn.relu(qkv[1]), jax.nn.relu(qkv[2]))
        attn = jnp.einsum('bhnd,bhmd->bhnm', q * SCALE, k)
        bias = rpb[idx].transpose(2, 0, 1)
        attn = attn + bias[None]
        attn = attn.reshape(-1, nW, NH, N, N) + mask[None, :, None]
        attn = attn.reshape(-1, NH, N, N)
        attn = jax.nn.softmax(jax.nn.relu(attn), axis=-1)
        out = jax.nn.relu(jnp.einsum('bhnm,bhmd->bhnd', attn, v))
        out = out.transpose(0, 2, 1, 3).reshape(-1, N, C) @ w_proj + b_proj
        xs = _rev(out)
        x = shortcut + jnp.roll(xs, (SH, SH), axis=(1, 2))
        h = jax.nn.gelu(_ln(x, gamma2, beta2) @ w_fc1 + b_fc1, approximate=False)
        return x + h @ w_fc2 + b_fc2

    def _L2_conv_ref(x, w1, b1, w2, b2):
        import jax, jax.numpy as jnp
        import numpy as np
        NUM_BLOCKS = 8
        HSF = 1
        LAMBDA = 0.01
        HTF = 1.0
        SCALE = 0.02

        def softshrink(v, lam):
            return jnp.where(v > lam, v - lam, jnp.where(v < -lam, v + lam, jnp.zeros_like(v)))
        B, H, W, C = x.shape
        nb = NUM_BLOCKS
        bs = C // nb
        Wf = W // 2 + 1
        bias = x
        xf = jnp.fft.rfft2(x.astype(jnp.float32), axes=(1, 2), norm='ortho')
        xf = xf.reshape(B, H, Wf, nb, bs)
        km = int((H // 2 + 1) * HTF)
        xk = xf[:, -km:, :km]
        xr, xi = (jnp.real(xk), jnp.imag(xk))
        o1r = jax.nn.relu(jnp.einsum('bhwni,nio->bhwno', xr, w1[0]) - jnp.einsum('bhwni,nio->bhwno', xi, w1[1]) + b1[0])
        o1i = jax.nn.relu(jnp.einsum('bhwni,nio->bhwno', xi, w1[0]) + jnp.einsum('bhwni,nio->bhwno', xr, w1[1]) + b1[1])
        o2r = jnp.einsum('bhwno,nok->bhwnk', o1r, w2[0]) - jnp.einsum('bhwno,nok->bhwnk', o1i, w2[1]) + b2[0]
        o2i = jnp.einsum('bhwno,nok->bhwnk', o1i, w2[0]) + jnp.einsum('bhwno,nok->bhwnk', o1r, w2[1]) + b2[1]
        o2r = softshrink(o2r, LAMBDA)
        o2i = softshrink(o2i, LAMBDA)
        full = jnp.zeros((B, H, Wf, nb, bs), dtype=jnp.complex64)
        full = full.at[:, -km:, :km].set(jax.lax.complex(o2r, o2i))
        full = full.reshape(B, H, Wf, C)
        out = jnp.fft.irfft2(full, s=(H, W), axes=(1, 2), norm='ortho').astype(x.dtype)
        return out + bias

    def _L3_conv_ref(x, mask_matrix, norm1_w, norm1_b, qkv_w, qkv_b, rpb_table, proj_w, proj_b, norm2_w, norm2_b, fc1_w, fc1_b, fc2_w, fc2_b):
        import jax, jax.numpy as jnp
        import numpy as np
        DIM = 256
        HEADS = 8
        WS = 8
        N = WS * WS
        NF = 2 * (N // 2 + 1)
        HD = DIM // HEADS
        SCALE = HD ** (-0.5)
        EPS = 1e-05

        def _rel_pos_index():
            ch = np.arange(WS)
            coords = np.stack(np.meshgrid(ch, ch, indexing='ij'))
            cf = coords.reshape(2, -1)
            rel = cf[:, :, None] - cf[:, None, :]
            rel = rel.transpose(1, 2, 0).astype(np.int64)
            rel[..., 0] += WS - 1
            rel[..., 1] += WS - 1
            rel[..., 0] *= 2 * WS - 1
            return jnp.asarray(rel.sum(-1))
        REL_IDX = _rel_pos_index()

        def _ln(x, w, b):
            m = jnp.mean(x, -1, keepdims=True)
            v = jnp.mean((x - m) ** 2, -1, keepdims=True)
            return (x - m) * jax.lax.rsqrt(v + EPS) * w + b

        def _attn_scores(t, qkv_w, qkv_b):
            Bw, Nt, C = t.shape
            qkv = (t @ qkv_w.T + qkv_b).reshape(Bw, Nt, 3, HEADS, HD)
            q, k, v = jnp.moveaxis(qkv, 2, 0)
            q = q.transpose(0, 2, 1, 3)
            k = k.transpose(0, 2, 1, 3)
            v = v.transpose(0, 2, 1, 3)
            a = jnp.einsum('bhnd,bhmd->bhnm', q, k) * SCALE
            return (a, v)
        B, H, W, C = x.shape
        shortcut = x
        x = _ln(x, norm1_w, norm1_b)
        xw = x.reshape(B, H // WS, WS, W // WS, WS, C).transpose(0, 1, 3, 2, 4, 5).reshape(-1, N, C)
        Bw = xw.shape[0]
        a, v = _attn_scores(xw, qkv_w, qkv_b)
        bias = rpb_table[REL_IDX.reshape(-1)].reshape(N, N, HEADS).transpose(2, 0, 1)
        a = jax.nn.softmax(a + bias[None], axis=-1)
        out = jnp.einsum('bhnm,bhmd->bhnd', a, v).transpose(0, 2, 1, 3).reshape(Bw, N, C)
        xf = jnp.fft.rfft(xw, axis=-2, norm='ortho')
        xf = jnp.concatenate([xf.real, xf.imag], axis=-2)
        af, vf = _attn_scores(xf, qkv_w, qkv_b)
        af = jax.nn.softmax(af, axis=-1)
        outf = jnp.einsum('bhnm,bhmd->bhnd', af, vf).transpose(0, 2, 1, 3).reshape(Bw, NF, C)
        cf = outf[:, :NF // 2] + 1j * outf[:, NF // 2:]
        xr = jnp.fft.irfft(cf, n=N, axis=-2, norm='ortho')
        xa = (out + xr) @ proj_w.T + proj_b
        x = xa.reshape(B, H // WS, W // WS, WS, WS, C).transpose(0, 1, 3, 2, 4, 5).reshape(B, H, W, C)
        x = shortcut + x
        h = _ln(x, norm2_w, norm2_b)
        h = jax.nn.gelu(h @ fc1_w.T + fc1_b, approximate=False)
        x = x + (h @ fc2_w.T + fc2_b)
        return x

    def _gn(v, G=32, eps=1e-5):
        B_, H_, W_, C_ = v.shape
        g = v.reshape(B_, H_, W_, G, C_ // G)
        m = jnp.mean(g, axis=(1, 2, 4), keepdims=True)
        s = jnp.var(g, axis=(1, 2, 4), keepdims=True)
        return ((g - m) / jnp.sqrt(s + eps)).reshape(v.shape)

    def _ln_c(v, eps=1e-6):
        m = jnp.mean(v, axis=-1, keepdims=True)
        s = jnp.var(v, axis=-1, keepdims=True)
        return (v - m) / jnp.sqrt(s + eps)

    def _ln_t(v, eps=1e-5):
        m = jnp.mean(v, axis=-1, keepdims=True)
        s = jnp.var(v, axis=-1, keepdims=True)
        return (v - m) / jnp.sqrt(s + eps)

    def _to_tokens(v):
        B_, H_, W_, C_ = v.shape
        return v.reshape(B_, H_ * W_, C_)
    def _from_tokens(t, like):
        return t.reshape(like.shape)

    x = _L0_conv_ref(x, L0_conv_w_in, L0_conv_b_in, L0_conv_w_dw, L0_conv_b_dw, L0_conv_ln_dw_g, L0_conv_ln_dw_b, L0_conv_w_off, L0_conv_b_off, L0_conv_w_mask, L0_conv_b_mask, L0_conv_w_out, L0_conv_b_out, L0_conv_ln1_g, L0_conv_ln1_b, L0_conv_w_fc1, L0_conv_b_fc1, L0_conv_w_fc2, L0_conv_b_fc2, L0_conv_ln2_g, L0_conv_ln2_b, L0_conv_gamma1, L0_conv_gamma2)
    x = _L1_conv_ref(x, L1_conv_gamma1, L1_conv_beta1, L1_conv_w_qkv, L1_conv_b_qkv, L1_conv_rpb, L1_conv_w_proj, L1_conv_b_proj, L1_conv_gamma2, L1_conv_beta2, L1_conv_w_fc1, L1_conv_b_fc1, L1_conv_w_fc2, L1_conv_b_fc2)
    x = _L2_conv_ref(x, L2_conv_w1, L2_conv_b1, L2_conv_w2, L2_conv_b2)
    x = _L3_conv_ref(x, L3_conv_mask_matrix, L3_conv_norm1_w, L3_conv_norm1_b, L3_conv_qkv_w, L3_conv_qkv_b, L3_conv_rpb_table, L3_conv_proj_w, L3_conv_proj_b, L3_conv_norm2_w, L3_conv_norm2_b, L3_conv_fc1_w, L3_conv_fc1_b, L3_conv_fc2_w, L3_conv_fc2_b)
    return x


_drawn_inputs = setup_inputs


def setup_inputs(seed=0):
    import zlib

    import numpy as np

    out = dict(_drawn_inputs(seed))
    spreads = {'L0_conv_b_in': (0.0, 0.1),
     'L0_conv_b_dw': (0.0, 0.308),
     'L0_conv_ln_dw_g': (1.0, 0.6),
     'L0_conv_ln_dw_b': (0.0, 0.8),
     'L0_conv_b_off': (0.0, 0.1),
     'L0_conv_b_out': (0.0, 0.1),
     'L0_conv_ln1_g': (1.0, 0.2),
     'L0_conv_ln1_b': (0.0, 0.1),
     'L0_conv_b_fc1': (0.0, 0.1),
     'L0_conv_b_fc2': (0.0, 0.1),
     'L0_conv_ln2_g': (1.0, 0.2),
     'L0_conv_ln2_b': (0.0, 0.1),
     'L0_conv_gamma1': (1.0, 0.2),
     'L0_conv_gamma2': (1.0, 0.2),
     'L1_conv_gamma1': (1.0, 0.6),
     'L1_conv_beta1': (0.0, 2.0),
     'L1_conv_b_qkv': (0.0, 0.794),
     'L1_conv_b_proj': (0.0, 0.1),
     'L1_conv_gamma2': (1.0, 0.6),
     'L1_conv_beta2': (0.0, 0.8),
     'L1_conv_b_fc1': (0.0, 0.384),
     'L1_conv_b_fc2': (0.0, 0.1),
     'L3_conv_mask_matrix': (0.0, 0.1),
     'L3_conv_norm1_w': (1.0, 0.6),
     'L3_conv_norm1_b': (0.0, 0.8),
     'L3_conv_qkv_b': (0.0, 0.296),
     'L3_conv_proj_b': (0.0, 0.1),
     'L3_conv_norm2_w': (1.0, 0.6),
     'L3_conv_norm2_b': (0.0, 0.8),
     'L3_conv_fc1_b': (0.0, 0.393),
     'L3_conv_fc2_b': (0.0, 0.1)}
    factors = {'L1_conv_rpb': 200.0,
     'L2_conv_w1': 8.0,
     'L2_conv_b1': 8.0,
     'L2_conv_w2': 8.0,
     'L2_conv_b2': 7.389,
     'L3_conv_rpb_table': 200.0}
    for name, (base, spread) in spreads.items():
        noise = np.random.default_rng([zlib.crc32(name.encode()), seed]).standard_normal(out[name].shape)
        drawn = base * np.exp(spread * noise) if base else spread * noise
        out[name] = jnp.asarray(drawn.astype(out[name].dtype))
    for name, factor in factors.items():
        out[name] = (out[name] * factor).astype(out[name].dtype)
    return out
```

```python
from contextlib import ExitStack
import numpy as np
import concourse.bass as bass
from concourse import mybir
from concourse.alu_op_type import AluOpType as ALU
ACT = mybir.ActivationFunctionType
AX = mybir.AxisListType
F32 = mybir.dt.float32
I32 = mybir.dt.int32
F32R = mybir.dt.float32r
P = 128
C = 256
KC = C // P
BATCH = 4
SIDE = 56
TOK = BATCH * SIDE * SIDE
BANK = 512
EPS = 1e-5
SHIFT = 3


def wait(eng, sem, value):
    if not (isinstance(value, int) and value <= 0):
        eng.wait_ge(sem, value)


def row_bc(ap, n):
    return ap.rearrange("(o c) -> o c", o=1).to_broadcast([n, ap.shape[0]])


def cols(ap):
    return ap.rearrange("(k p) -> p k", p=P)


def spread(ap, n):
    return ap.rearrange("p (o c) -> p o c", o=1).to_broadcast([ap.shape[0], n, ap.shape[1]])


def along(ap, n):
    return ap.rearrange("p (g o) -> p g o", o=1).to_broadcast([ap.shape[0], ap.shape[1], n])


def by_pairs(count, body):
    def run(eng):
        for n in range(2):
            body(n, n % 2, 0)
        with eng.Fori(1, count // 2 - 1) as i:
            for k in range(2):
                body(i * 2 + k, k, i)
        for n in range(count - 2, count):
            body(n, n % 2, n // 2)
    return run


def next_of(n, k, i):
    return n + 1, 1 - k, i + k


def hold(eng, passed):
    eng.sem_inc(passed, 1)


def close_phase(nc, sems):
    nc.clear_and_free_semaphores(sems)
    nc.all_engine_barrier()


def cut(v, high, whole):
    return v.tensor_copy(high.bitcast(F32R), whole)


def rest(v, low, whole, high):
    return v.tensor_tensor(low.bitcast(F32R), whole, high, ALU.subtract)


def split_product(pe, to, left, right, first, last):
    (lh, ll), (rh, rl) = [[a.bitcast(F32R) for a in side] for side in (left, right)]
    pe.matmul(to, lh, rh, start=first, stop=False)
    pe.matmul(to, lh, rl, start=False, stop=False)
    return pe.matmul(to, ll, rh, start=False, stop=last)


COLS = 8
CHUNKS = SIDE // COLS
NCH = 2 * CHUNKS
PIX = 2 * SIDE
TAPS = 9
GROUPS = 16
OM = 3 * TAPS * GROUPS
MARGIN = 3
WIDE = SIDE + 2 * MARGIN


def dcn_front(nc, x, xp, om, reach, w_in, b_in, w_dw, b_dw, gain, bias, w_om, b_om, ident):
    FOUR = COLS // 2
    NB = FOUR * PIX
    xv = x.rearrange("(h r g j) c -> h g r (j c)", h=2, r=PIX, g=CHUNKS)
    xpv = xp.rearrange("(h x b y) c -> h b y x c", h=2, x=WIDE, b=2)
    omv = om.rearrange("(n j p) o -> n p j o", j=COLS, p=PIX)
    with ExitStack() as ctx:
        def sb(name, shape):
            return ctx.enter_context(nc.sbuf_tensor(f"fr_{name}", shape, F32))

        def ps(name, shape):
            return ctx.enter_context(nc.psum_tensor(f"fr_{name}", shape, F32))

        sems = []

        def sem(name):
            sems.append(nc.alloc_semaphore(f"fr_{name}"))
            return sems[-1]

        id_sb = sb("id", [P, P])
        wi_sb = sb("wi", [P, KC, C])
        wo_sb = sb("wo", [P, KC, OM])
        wd_sb = sb("wd", [P, KC, TAPS])
        bd_sb = sb("bd", [P, KC])
        gin = sb("gin", [P, KC])
        bin_ = sb("bin", [P, KC])
        bi_bc = sb("bi", [PIX, C])
        bo_bc = sb("bo", [PIX, OM])
        half = sb("half", [PIX, COLS])
        zero = sb("zero", [WIDE, 2 * MARGIN, C])
        xin = sb("xin", [PIX, 2, COLS, C])
        xT = sb("xT", [P, KC, COLS, PIX])
        cb = sb("cb", [P, KC, SIDE + 2, 2, SIDE + 2])
        xps = sb("xps", [PIX, 2, COLS, C])
        acc = sb("acc", [P, 2, KC, COLS, PIX])
        tok = sb("tok", [PIX, COLS, C])
        amax = sb("amax", [PIX, 2 * SIDE])
        stats = sb("stats", [PIX, COLS, 6])
        mv = sb("mv", [PIX, COLS, 2])
        rstd = sb("rstd", [PIX, COLS])
        x1T = sb("x1T", [P, KC, COLS, PIX])
        oms = sb("oms", [PIX, 2, COLS, OM])
        t_ps = ps("t_ps", [P, 2, BANK])
        i_ps = ps("i_ps", [P, 2, BANK])
        b_ps = ps("b_ps", [P, 2, BANK])
        o_ps = ps("o_ps", [P, 2, BANK])

        w_ready = sem("w_ready")
        zeroed = sem("zeroed")
        consts = sem("consts")
        margins = sem("margins")
        passed = sem("passed")
        warm = sem("warm")
        x_ready = [sem(f"x_ready{k}") for k in range(2)]
        t_made = sem("t_made")
        t_taken = sem("t_taken")
        i_made = sem("i_made")
        i_taken = sem("i_taken")
        b_made = sem("b_made")
        b_taken = sem("b_taken")
        o_made = sem("o_made")
        o_taken = sem("o_taken")
        conv = sem("conv")
        ln = sem("ln")
        var_ready = sem("var_ready")
        rstd_ready = sem("rstd_ready")
        normed = sem("normed")
        biased = sem("biased")
        reached = sem("reached")
        reach_stored = sem("reach_stored")
        xp_stored = [sem(f"xp_stored{k}") for k in range(2)]
        om_stored = [sem(f"om_stored{k}") for k in range(2)]
        WLOADS = 9
        NCONV = TAPS * KC
        ctx.callback(close_phase, nc, sems)
        block = ctx.enter_context(nc.Block())

        def more(n):
            return not (isinstance(n, int) and n + 1 >= NCH)

        def whole(n):
            return not (isinstance(n, int) and n < 1)

        def prev_of(n, k, i):
            return n - 1, 1 - k, i - 1 + k

        def turn_use(n):
            if isinstance(n, int):
                return n * 4 if n < 2 else n * 8 - 8
            return n * 8 - 8

        def norm_use(n):
            return (n * 8 + 12) if not (isinstance(n, int) and n >= NCH - 2) else norm_last(n)

        def norm_last(n):
            return (NCH - 3) * 8 + 16 + (n - (NCH - 2)) * 4

        @block.sync
        def _(sp):
            def load(n, k):
                sp.dma_start(xin[:, k].rearrange("p j c -> p (j c)"), xv[n // CHUNKS, n % CHUNKS]).then_inc(x_ready[k], 16)

            for k in range(2):
                sp.sem_inc(om_stored[k], 1)
            load(0, 0)
            load(1, 1)
            for dst, src in ((id_sb[:], ident), (wi_sb[:], w_in.rearrange("(k p) n -> p k n", p=P)),
                             (wo_sb[:], w_om.rearrange("(k p) n -> p k n", p=P)), (bi_bc[:], row_bc(b_in, PIX)),
                             (bo_bc[:], row_bc(b_om, PIX))):
                sp.dma_start(dst, src).then_inc(w_ready, 16)
            with nc.allow_non_contiguous_dma(reason="bias columns"):
                sp.dma_start(wd_sb[:], w_dw.rearrange("(k p) t -> p k t", p=P)).then_inc(w_ready, 16)
                for dst, src in ((bd_sb, b_dw), (gin, gain), (bin_, bias)):
                    sp.dma_start(dst[:], cols(src)).then_inc(w_ready, 16)
            sp.wait_ge(zeroed, 3)
            n_margin = 0
            for h in range(2):
                for b in range(2):
                    for x0 in (0, WIDE - MARGIN):
                        sp.dma_start(xpv[h, b, :, x0:x0 + MARGIN], zero[:, 0:MARGIN]).then_inc(margins, 16)
                        n_margin += 1
                    for y0 in (0, WIDE - MARGIN):
                        dst = xpv[h, b, y0:y0 + MARGIN, MARGIN:WIDE - MARGIN].rearrange("y x c -> x y c")
                        sp.dma_start(dst, zero[0:SIDE, 0:MARGIN]).then_inc(margins, 16)
                        n_margin += 1

            def store_xp(n, k):
                wait(sp, i_taken, n * 4 + 4)
                for b in range(2):
                    x0 = (n % CHUNKS) * COLS + MARGIN
                    dst = xpv[n // CHUNKS, b, MARGIN:MARGIN + SIDE, bass.ds(x0, COLS)]
                    sp.dma_start(dst, xps[b * SIDE:(b + 1) * SIDE, k]).then_inc(xp_stored[k], 16)

            def body(n, k, i):
                if not (isinstance(n, int) and n + 2 >= NCH):
                    wait(sp, t_made, turn_use(n) + 4)
                    load(n + 2, k)
                if more(n):
                    m, q, _ = next_of(n, k, i)
                    store_xp(m, q)
                if whole(n):
                    m, q, _ = prev_of(n, k, i)
                    wait(sp, biased, (m + 1) * (COLS // 2))
                    sp.dma_start(omv[m], oms[:, q]).then_inc(om_stored[q], 16)

            store_xp(0, 0)
            by_pairs(NCH, body)(sp)
            sp.wait_ge(biased, NCH * (COLS // 2))
            sp.dma_start(omv[NCH - 1], oms[:, 1]).then_inc(om_stored[1], 16)
            sp.wait_ge(reached, NCH + 1)
            sp.dma_start(reach, amax[:]).then_inc(reach_stored, 16)
            sp.wait_ge(reach_stored, 16)
            sp.wait_ge(margins, 16 * n_margin)
            for k in range(2):
                sp.wait_ge(xp_stored[k], 16 * NCH)
                sp.wait_ge(om_stored[k], 16 * NCH // 2 + 1)

        @block.gpsimd
        def _(pool):
            pool.memset(zero[:], 0.0).then_inc(zeroed, 1)
            pool.memset(cb[:], 0.0).then_inc(zeroed, 1)
            pool.memset(half[:], -0.5).then_inc(zeroed, 1)
            pool.wait_ge(zeroed, 3)
            pool.wait_ge(w_ready, 16 * WLOADS)

            def back(n, k):
                pool.wait_ge(var_ready, n + 1)
                pool.tensor_tensor(rstd[:], mv[:, :, 1], half[:], ALU.pow).then_inc(rstd_ready, 1)
                for j in range(0, COLS, 2):
                    pool.wait_ge(o_taken, n * COLS + j + 2)
                    pool.tensor_tensor(oms[:, k, j:j + 2], oms[:, k, j:j + 2], spread(bo_bc[:], 2), ALU.add).then_inc(biased, 1)

            def body(n, k, i):
                if whole(n):
                    back(n - 1, 1 - k)

            by_pairs(NCH, body)(pool)
            back(NCH - 1, 1)

        @block.vector
        def _(v):
            v.wait_ge(w_ready, 16 * WLOADS)
            v.wait_ge(zeroed, 3)
            v.sem_inc(reached, 1)

            def take_xp(n, k, i, part):
                wait(v, xp_stored[k], i * 32)
                for j in part:
                    v.wait_ge(i_made, n * 4 + j + 1)
                    v.tensor_tensor(xps[:, k, 2 * j:2 * j + 2], i_ps[0:PIX, j % 2].rearrange("p (j c) -> p j c", c=C),
                                    spread(bi_bc[:], 2), ALU.add).then_inc(i_taken, 1)

            def convolve(n, k):
                if more(n):
                    wait(v, t_taken, turn_use(n + 1) + 4)
                wait(v, b_made, (n - 1) * 4)
                x0 = (n % CHUNKS) * COLS
                for t in range(TAPS):
                    for c in range(KC):
                        src = cb[:, c, bass.ds(x0 + t % 3, COLS), :, t // 3:t // 3 + SIDE]
                        dst = acc[:, k, c].rearrange("p x (b y) -> p x b y", b=2)
                        if t == 0:
                            v.tensor_scalar(dst, src, wd_sb[:, c, 0:1], bd_sb[:, c:c + 1], ALU.mult, ALU.add).then_inc(conv, 1)
                            continue
                        v.wait_ge(conv, n * NCONV + (t - 1) * KC + c + 1)
                        v.scalar_tensor_tensor(out=dst, in0=src, scalar=wd_sb[:, c, t:t + 1], in1=dst, op0=ALU.mult,
                                               op1=ALU.add).then_inc(conv, 1)

            def norm(n):
                v.wait_ge(b_taken, n * 4 + 4)
                for j in range(COLS):
                    ins = v.bn_stats(stats[:, j], tok[:, j])
                ins.then_inc(ln, 1)
                v.wait_ge(ln, n * 2 + 1)
                hold(v, passed)
                for j in range(COLS):
                    ins = v.bn_aggr(mv[:, j], stats[:, j])
                ins.then_inc(ln, 1)
                v.wait_ge(ln, n * 2 + 2)
                v.tensor_scalar(mv[:, :, 1], mv[:, :, 1], EPS, None, ALU.add).then_inc(var_ready, 1)
                v.wait_ge(rstd_ready, n + 1)
                v.wait_ge(var_ready, n + 1)
                for j in range(COLS):
                    ins = v.tensor_scalar(tok[:, j], tok[:, j], mv[:, j, 0:1], rstd[:, j:j + 1], ALU.subtract, ALU.mult)
                ins.then_inc(normed, 1)

            def measure(n, k):
                v.wait_ge(biased, (n + 1) * (COLS // 2))
                v.tensor_reduce(amax[:, bass.ds(n * COLS, COLS)], oms[:, k, :, 0:2 * TAPS * GROUPS], AX.X, ALU.max,
                                apply_absolute_value=True).then_inc(reached, 1)

            def body(n, k, i):
                if more(n):
                    take_xp(*next_of(n, k, i), (0, 1))
                if not (isinstance(n, int) and n < 2):
                    measure(n - 2, k)
                if whole(n):
                    norm(n - 1)
                if more(n):
                    take_xp(*next_of(n, k, i), (2, 3))
                convolve(n, k)

            take_xp(0, 0, 0, range(4))
            by_pairs(NCH, body)(v)
            norm(NCH - 1)
            for n in range(NCH - 2, NCH):
                measure(n, n % 2)

        @block.scalar
        def _(act):
            act.wait_ge(w_ready, 16 * WLOADS)
            act.wait_ge(zeroed, 3)
            act.activation(rstd[:, 0:1], bi_bc[:, 0:1], ACT.Gelu).then_inc(warm, 1)
            act.wait_ge(warm, 1)

            def take_turned(n):
                wait(act, i_made, n * 4)
                wait(act, conv, (n - 2) * NCONV)
                x0 = (n % CHUNKS) * COLS + 1
                for u in range(4):
                    f, c = u // 2, u % 2
                    wait(act, t_made, turn_use(n) + u + 1)
                    src = t_ps[:, u % 2, 0:NB]
                    act.activation(xT[:, c, f * FOUR:(f + 1) * FOUR].rearrange("p j r -> p (j r)"), src, ACT.Copy)
                    act.activation(cb[:, c, bass.ds(x0 + f * FOUR, FOUR), :, 1:SIDE + 1],
                                   src.rearrange("p (j b y) -> p j b y", j=FOUR, b=2), ACT.Copy).then_inc(t_taken, 1)

            def take_conv(n):
                if whole(n):
                    wait(act, t_made, norm_use(n - 1) + 4)
                for j in range(4):
                    act.wait_ge(b_made, n * 4 + j + 1)
                    act.activation(tok[:, 2 * j:2 * j + 2].rearrange("p j c -> p (j c)"), b_ps[0:PIX, j % 2], ACT.Copy)\
                        .then_inc(b_taken, 1)

            def back(n, k, i):
                wait(act, o_made, n * COLS)
                for u in range(4):
                    f, c = u // 2, u % 2
                    wait(act, t_made, norm_use(n) + u + 1)
                    act.activation(x1T[:, c, f * FOUR:(f + 1) * FOUR].rearrange("p j r -> p (j r)"), t_ps[:, u % 2, 0:NB],
                                   ACT.Gelu, bias=bin_[:, c:c + 1], scale=gin[:, c:c + 1]).then_inc(t_taken, 1)
                act.wait_ge(om_stored[k], i * 16 + 1)
                wait(act, reached, n)
                for j in range(COLS):
                    act.wait_ge(o_made, n * COLS + j + 1)
                    act.activation(oms[:, k, j], o_ps[0:PIX, j % 2, 0:OM], ACT.Copy).then_inc(o_taken, 1)

            def body(n, k, i):
                if more(n):
                    take_turned(n + 1)
                if whole(n):
                    take_conv(n - 1)
                if whole(n):
                    back(*prev_of(n, k, i))

            take_turned(0)
            by_pairs(NCH, body)(act)
            take_conv(NCH - 1)
            back(NCH - 1, 1, NCH // 2 - 1)

        @block.tensor
        def _(pe):
            pe.wait_ge(w_ready, 16 * WLOADS)

            def turn(n, k, i):
                pe.wait_ge(x_ready[k], i * 16 + 16)
                for u in range(4):
                    f, c = u // 2, u % 2
                    wait(pe, t_taken, turn_use(n) + u - 1)
                    for j in range(FOUR):
                        ins = pe.transpose(t_ps[:, u % 2, j * PIX:(j + 1) * PIX], xin[:, k, f * FOUR + j, c * P:(c + 1) * P],
                                           id_sb[0:PIX, 0:PIX])
                    ins.then_inc(t_made, 1)

            def enter(n, part):
                wait(pe, t_taken, turn_use(n) + 4)
                for j in part:
                    wait(pe, i_taken, n * 4 + j - 1)
                    for q in range(2):
                        for c in range(KC):
                            ins = pe.matmul(i_ps[0:PIX, j % 2, q * C:(q + 1) * C], xT[:, c, 2 * j + q], wi_sb[:, c],
                                            start=(c == 0), stop=(c == KC - 1))
                    ins.then_inc(i_made, 1)

            def turn_conv(n, k):
                pe.wait_ge(conv, n * NCONV + NCONV)
                for j in range(4):
                    wait(pe, b_taken, n * 4 + j - 1)
                    for q in range(2):
                        for c in range(KC):
                            ins = pe.transpose(b_ps[0:PIX, j % 2, (q * KC + c) * P:(q * KC + c + 1) * P],
                                               acc[:, k, c, 2 * j + q], id_sb[:])
                    ins.then_inc(b_made, 1)

            def back(n):
                pe.wait_ge(normed, n + 1)
                for u in range(4):
                    f, c = u // 2, u % 2
                    wait(pe, t_taken, norm_use(n) + u - 1)
                    for j in range(FOUR):
                        ins = pe.transpose(t_ps[:, u % 2, j * PIX:(j + 1) * PIX], tok[:, f * FOUR + j, c * P:(c + 1) * P],
                                           id_sb[0:PIX, 0:PIX])
                    ins.then_inc(t_made, 1)
                wait(pe, t_taken, norm_use(n) + 4)
                for j in range(COLS):
                    wait(pe, o_taken, n * COLS + j - 1)
                    for c in range(KC):
                        ins = pe.matmul(o_ps[0:PIX, j % 2, 0:OM], x1T[:, c, j], wo_sb[:, c], start=(c == 0),
                                        stop=(c == KC - 1))
                    ins.then_inc(o_made, 1)

            def body(n, k, i):
                if more(n):
                    turn(*next_of(n, k, i))
                    enter(n + 1, (0, 1))
                if whole(n):
                    turn_conv(n - 1, 1 - k)
                if more(n):
                    enter(n + 1, (2, 3))
                if whole(n):
                    back(n - 1)

            turn(0, 0, 0)
            enter(0, range(4))
            by_pairs(NCH, body)(pe)
            turn_conv(NCH - 1, 1)
            back(NCH - 1)


NCOL = 2 * SIDE
GC = C // GROUPS
KG = TAPS * GROUPS
REACH = 2
SH = 2 * REACH + 1
SPAN = SH + 2
RUN = SPAN * C
FOLDED = (1, 3, 5)
FOLD = 2
RING = 8


def places():
    taps = np.arange(TAPS)
    own = np.stack([np.tile(np.arange(SIDE), 2), np.repeat([0, WIDE], SIDE)], 1)
    rest = np.concatenate([np.arange(NCOL) % SIDE, np.repeat(taps % 3 - 1, GROUPS), np.repeat(taps // 3 - 1, GROUPS),
                           np.tile(np.arange(GROUPS), TAPS)])
    return np.concatenate([own, np.broadcast_to(rest, (PIX, rest.size))], 1).astype(np.float32)


def dcn_sample(nc, xp, om, reach, x, out, w_out, b_out, gain, bias, factor, ident, place, limit=float(REACH)):
    xv = x.rearrange("(h r g j) c -> h g r (j c)", h=2, r=PIX, g=CHUNKS)
    ov = out.rearrange("(b r j) c -> b r (j c)", b=BATCH, r=SIDE)
    omv = om.rearrange("(n p) o -> n p o", p=PIX)
    with ExitStack() as ctx:
        def sb(name, shape, kind=F32):
            return ctx.enter_context(nc.sbuf_tensor(f"sa_{name}", shape, kind))

        def ps(name, shape):
            return ctx.enter_context(nc.psum_tensor(f"sa_{name}", shape, F32))

        sems = []

        def sem(name):
            sems.append(nc.alloc_semaphore(f"sa_{name}"))
            return sems[-1]

        id_sb = sb("id", [P, P])
        wo_sb = sb("wo", [P, KC, C])
        bo_bc = sb("bo", [PIX, C])
        gain_bc = sb("gain", [PIX, C])
        bias_bc = sb("bias", [PIX, C])
        fac_bc = sb("fac", [PIX, C])
        half = sb("half", [PIX, 1])
        shift = sb("shift", [PIX, SH + 1])
        nil = sb("nil", [PIX, 1])
        reach_sb = sb("reach", [PIX, NCOL])
        most = sb("most", [PIX, 1])
        far = sb("far", [1, NCOL], I32)
        v_sb = sb("v", [PIX, RING, RUN])
        prod = sb("prod", [PIX, RING, RUN])
        om_sb = sb("om", [PIX, 4, OM])
        hat = sb("hat", [PIX, 2, SH, 2 * KG])
        hatm = sb("hatm", [PIX, 2, SH, KG])
        most_g = sb("most_g", [PIX, GROUPS])
        mask = sb("mask", [PIX, 4, KG])
        total = sb("total", [PIX, GROUPS])
        wt = sb("wt", [PIX, 2, SPAN, SPAN, GROUPS])
        part = sb("part", [PIX, 2, SH, SH, GROUPS])
        yT = sb("yT", [P, 2, KC, PIX])
        tok = sb("tok", [PIX, 4, C])
        res = sb("res", [PIX, COLS, C])
        stats = sb("stats", [PIX, 2, 6])
        mv = sb("mv", [PIX, 2, 2])
        rstd = sb("rstd", [PIX, 2])
        place_sb = sb("place", [PIX, 2 + NCOL + 3 * KG])
        g_off = sb("g_off", [PIX, 2 * KG])
        g_col = sb("g_col", [PIX, 1])
        g_low = sb("g_low", [PIX, 2, KG])
        g_frac = sb("g_frac", [PIX, 2, KG])
        g_over = sb("g_over", [PIX, KG])
        g_int = sb("g_int", [PIX, KG], I32)
        g_w = sb("g_w", [PIX, 4, KG])
        g_now = sb("g_now", [PIX, GROUPS], I32)
        g_got = sb("g_got", [PIX, 4, C])
        g_sum = sb("g_sum", [PIX, C])
        y_ps = ps("y_ps", [P, 2, KC, BANK])
        o_ps = ps("o_ps", [P, 2, BANK])

        w_ready = sem("w_ready")
        consts = sem("consts")
        warm = sem("warm")
        passed = sem("passed")
        tested = sem("tested")
        om_ready = [sem(f"om_ready{q}") for q in range(4)]
        v_ready = [sem(f"v_ready{q}") for q in range(RING)]
        x_ready = [sem(f"x_ready{q}") for q in range(2)]
        stored = [sem(f"stored{q}") for q in range(2)]
        distanced = sem("distanced")
        hatted = sem("hatted")
        maxed = sem("maxed")
        centred = sem("centred")
        exped = sem("exped")
        summed = sem("summed")
        inverted = sem("inverted")
        masked = sem("masked")
        weighted = sem("weighted")
        cleared = sem("cleared")
        built = sem("built")
        multiplied = sem("multiplied")
        made = sem("made")
        used = sem("used")
        approved = sem("approved")
        y_taken = sem("y_taken")
        o_made = sem("o_made")
        o_taken = sem("o_taken")
        statted = sem("statted")
        aggred = sem("aggred")
        var_ready = sem("var_ready")
        rstd_ready = sem("rstd_ready")
        scaled = sem("scaled")
        added = sem("added")
        finished = sem("finished")
        g_step = sem("g_step")
        g_dma = sem("g_dma")
        WLOADS = 8
        BUILDS = 2 * TAPS
        ctx.callback(close_phase, nc, sems)
        block = ctx.enter_context(nc.Block())

        def walk(body, enter=None):
            def run(eng):
                if enter:
                    enter(0)
                body(0, 0)
                with eng.Fori(1, CHUNKS) as n:
                    body(n, 0)
                if enter:
                    enter(1)
                with eng.Fori(CHUNKS, NCH - 1) as n:
                    body(n, 1)
                body(NCH - 1, 1)
            return run

        def near(n, j, d):
            m, q = n + (j + d) // COLS, (j + d) % COLS
            if isinstance(n, int) and not 0 <= m < NCH:
                return None
            return m * COLS + q, q

        @block.sync
        def _(sp):
            def load_om(g, q):
                wait(sp, hatted, g - 3)
                wait(sp, centred, g - 3)
                sp.dma_start(om_sb[:, q % 4], omv[g]).then_inc(om_ready[q % 4], 16)

            def load_v(h, c, slot):
                for b in range(2):
                    first = (((c + h * WIDE) * 2 + b) * WIDE) * C
                    sp.dma_start(v_sb[b * SIDE:(b + 1) * SIDE, slot], bass.AP(xp.tensor, first, [[C, SIDE], [1, RUN]]))\
                        .then_inc(v_ready[slot], 16)

            def load_x(n, a):
                cols_of = slice(a * COLS // 2 * C, (a + 1) * COLS // 2 * C)
                sp.dma_start(res[:, a * COLS // 2:(a + 1) * COLS // 2].rearrange("p j c -> p (j c)"),
                             xv[n // CHUNKS, n % CHUNKS][:, cols_of]).then_inc(x_ready[a], 16)

            def store(n, a):
                wait(sp, finished, n * COLS + (a + 1) * (COLS // 2))
                src = res[:, a * COLS // 2:(a + 1) * COLS // 2].rearrange("p j c -> p (j c)")
                w = COLS // 2 * C
                c0 = (n % CHUNKS) * COLS * C + a * w
                for b in range(2):
                    for y0, y1, r0 in ((SHIFT, SIDE, 0), (0, SHIFT, SIDE - SHIFT)):
                        dst = ov[(n // CHUNKS) * 2 + b, r0:r0 + y1 - y0, bass.ds(c0, w)]
                        sp.dma_start(dst, src[b * SIDE + y0:b * SIDE + y1]).then_inc(stored[a], 16)

            def enter(h):
                if h == 0:
                    for g in range(2):
                        load_om(g, g)
                    for a in range(2):
                        load_x(0, a)
                for c in range(SPAN - 1):
                    if h:
                        wait(sp, made, (SIDE - 1) * SPAN + c + 2)
                    load_v(h, c, c)

            def body(n, h):
                for j in range(COLS):
                    g = n * COLS + j
                    ahead = near(n, j, 2)
                    if ahead:
                        load_om(*ahead)
                    wait(sp, made, (g - 2) * SPAN + 1)
                    load_v(h, (n - h * CHUNKS) * COLS + (j + SPAN - 1), (j + SPAN - 1) % RING)
                    later = not (isinstance(n, int) and n == 0)
                    if later and j == 0:
                        store(n - 1, 0)
                    if later and j == 1:
                        sp.wait_ge(stored[0], n * 64)
                        load_x(n, 0)
                    if later and j == 5:
                        store(n - 1, 1)
                    if later and j == 6:
                        sp.wait_ge(stored[1], n * 64)
                        load_x(n, 1)

            for dst, src in ((id_sb[:], ident), (wo_sb[:], w_out.rearrange("(k p) n -> p k n", p=P)), (bo_bc[:], row_bc(b_out, PIX)),
                             (gain_bc[:], row_bc(gain, PIX)), (bias_bc[:], row_bc(bias, PIX)), (fac_bc[:], row_bc(factor, PIX)),
                             (reach_sb[:], reach), (place_sb[:], place)):
                sp.dma_start(dst, src).then_inc(w_ready, 16)
            walk(body, enter)(sp)
            for a in range(2):
                store(NCH - 1, a)
                sp.wait_ge(stored[a], NCH * 64)

        @block.gpsimd
        def _(pool):
            pool.memset(half[:], -0.5).then_inc(consts, 1)
            pool.memset(nil[:], 0.0).then_inc(consts, 1)
            for s in range(SH):
                pool.memset(shift[:, s:s + 1], float(REACH - s)).then_inc(consts, 1)
            pool.memset(shift[:, SH:SH + 1], 1.0).then_inc(consts, 1)
            pool.wait_ge(w_ready, 16 * WLOADS)
            pool.tensor_tensor(gain_bc[:], gain_bc[:], fac_bc[:], ALU.mult).then_inc(consts, 1)
            pool.tensor_tensor(bias_bc[:], bias_bc[:], fac_bc[:], ALU.mult).then_inc(consts, 1)
            pool.wait_ge(consts, SH + 5)
            pool.wait_ge(tested, 4)

            def build(g, q):
                base = g * BUILDS
                two = q % 2
                pool.wait_ge(weighted, g + 1)
                wait(pool, built, base)

                def multiply(k):
                    if k > 1:
                        pool.wait_ge(built, base + 2 * k - 1)
                    gx = hat[:, two, :, k * GROUPS:(k + 1) * GROUPS].rearrange("p s (o g) -> p s o g", o=1)
                    gy = hatm[:, two, :, k * GROUPS:(k + 1) * GROUPS].rearrange("p (o s) g -> p o s g", o=1)
                    shape = [PIX, SH, SH, GROUPS]
                    pool.tensor_tensor(part[:, k % 2], gx.to_broadcast(shape), gy.to_broadcast(shape), ALU.mult).then_inc(built, 1)

                def add(k):
                    if k == 0:
                        pool.wait_ge(cleared, g + 1)
                    pool.wait_ge(built, base + 2 * k + 1)
                    ky, kx = k // 3, k % 3
                    dst = wt[:, two, kx:kx + SH, ky:ky + SH]
                    pool.tensor_tensor(dst, dst, part[:, k % 2], ALU.add).then_inc(built, 1)

                multiply(0)
                for k in range(1, TAPS):
                    multiply(k)
                    add(k - 1)
                add(TAPS - 1)

            def root(g, q):
                pool.wait_ge(var_ready, g + 1)
                two = q % 2
                pool.tensor_tensor(rstd[:, two:two + 1], mv[:, two, 1:2], half[:], ALU.pow).then_inc(rstd_ready, 1)

            def body(n, h):
                for j in range(COLS):
                    g = n * COLS + j
                    build(g, j)
                    back = near(n, j, -3)
                    if back:
                        root(*back)
                    approve(g, j, h)

            def general(g, q, h):
                steps = [0]

                def then(ins):
                    steps[0] += 1
                    ins.then_inc(g_step, 1)
                    pool.wait_ge(g_step, steps[0])

                def fresh():
                    pool.dma_reset(range(g_dma.num, g_dma.num + 1))
                    pool.sem_clear(g_dma)

                pool.sem_clear(g_step)
                fresh()
                pool.dma_start(g_off[:], omv[g][:, 0:2 * KG]).then_inc(g_dma, 16)
                pool.wait_ge(g_dma, 16)
                then(pool.tensor_copy(g_col[:], place_sb[:, bass.ds(g + 2, 1)]))
                for a in range(2):
                    low, frac = g_low[:, a], g_frac[:, a]
                    tap = place_sb[:, 2 + NCOL + a * KG:2 + NCOL + (a + 1) * KG]
                    here = g_col[:] if a == 0 else place_sb[:, 0:1]
                    then(pool.tensor_scalar(frac, tap, here, None, ALU.add))
                    then(pool.tensor_tensor(frac, frac, g_off[:, a * KG:(a + 1) * KG], ALU.add))
                    then(pool.tensor_scalar(frac, frac, 2.0, 0.0, ALU.add, ALU.max))
                    then(pool.tensor_scalar(frac, frac, float(SIDE + 3), None, ALU.min))
                    then(pool.tensor_copy(g_int[:], frac))
                    then(pool.tensor_copy(low, g_int[:]))
                    then(pool.tensor_tensor(g_over[:], low, frac, ALU.subtract))
                    then(pool.tensor_scalar(g_over[:], g_over[:], 0.0, None, ALU.is_gt))
                    then(pool.tensor_tensor(low, low, g_over[:], ALU.subtract))
                    then(pool.tensor_tensor(frac, frac, low, ALU.subtract))
                then(pool.tensor_tensor(g_w[:, 3], g_frac[:, 0], g_frac[:, 1], ALU.mult))
                then(pool.tensor_tensor(g_w[:, 2], g_frac[:, 0], g_w[:, 3], ALU.subtract))
                then(pool.tensor_tensor(g_w[:, 1], g_frac[:, 1], g_w[:, 3], ALU.subtract))
                then(pool.tensor_scalar(g_frac[:, 0], g_frac[:, 0], -1.0, 1.0, ALU.mult, ALU.add))
                then(pool.tensor_tensor(g_w[:, 0], g_frac[:, 0], g_w[:, 1], ALU.subtract))
                for c in range(4):
                    then(pool.tensor_tensor(g_w[:, c], g_w[:, c], mask[:, q % 4], ALU.mult))
                then(pool.tensor_scalar(g_low[:, 0], g_low[:, 0], float(h * WIDE + 1), float(2 * WIDE), ALU.add, ALU.mult))
                then(pool.tensor_tensor(g_low[:, 0], g_low[:, 0], g_low[:, 1], ALU.add))
                then(pool.tensor_scalar(g_low[:, 0], g_low[:, 0], place_sb[:, 1:2], None, ALU.add))
                then(pool.tensor_scalar(g_low[:, 0], g_low[:, 0], 1.0, float(GROUPS), ALU.add, ALU.mult))
                then(pool.tensor_tensor(g_low[:, 0], g_low[:, 0], place_sb[:, 2 + NCOL + 2 * KG:2 + NCOL + 3 * KG], ALU.add))
                then(pool.tensor_copy(g_int[:], g_low[:, 0]))
                then(pool.memset(g_sum[:], 0.0))
                xg = xp.rearrange("n (g c) -> (n g) c", c=GC)
                with pool.Fori(0, TAPS) as k:
                    pool.sem_clear(g_step)
                    fresh()
                    steps[0] = 0
                    then(pool.tensor_copy(g_now[:], g_int[:, bass.ds(k * GROUPS, GROUPS)]))
                    for c in range(4):
                        for s in range(GROUPS):
                            first = ((c // 2) * 2 * WIDE + c % 2) * C
                            pool.indirect_dma_start(
                                out=g_got[:, c, s * GC:(s + 1) * GC], out_offset=None, in_=xg,
                                in_offset=bass.IndirectOffsetOnAxis(ap=g_now[:, s:s + 1], axis=0),
                                element_offset=first).then_inc(g_dma, 16)
                    pool.wait_ge(g_dma, 4 * GROUPS * 16)
                    for c in range(4):
                        got = g_got[:, c].rearrange("p (s e) -> p s e", e=GC)
                        w = along(g_w[:, c, bass.ds(k * GROUPS, GROUPS)], GC)
                        then(pool.tensor_tensor(got, got, w, ALU.mult))
                        then(pool.tensor_tensor(g_sum[:], g_sum[:], g_got[:, c], ALU.add))
                pool.wait_ge(made, g * SPAN + SPAN)
                hold(pool, passed)
                pool.sem_clear(g_step)
                steps[0] = 0
                for dx in range(SPAN):
                    then(pool.memset(prod[:, (q * SPAN + dx) % RING], 0.0))
                then(pool.tensor_copy(prod[:, (q * SPAN) % RING, 0:C], g_sum[:]))

            def approve(g, q, h):
                beyond = pool.value_load(far[0:1, bass.ds(g, 1)], min_val=0, max_val=1)
                with pool.If(beyond > 0):
                    general(g, q, h)
                pool.sem_inc(approved, 1)

            walk(body)(pool)
            for g in range(NCOL - 3, NCOL):
                root(g, g % COLS)

        @block.vector
        def _(v):
            v.wait_ge(w_ready, 16 * WLOADS)
            v.wait_ge(consts, SH + 5)
            v.wait_ge(tested, 1)
            v.tensor_reduce(most[:], o_ps[0:NCOL, 0, 0:PIX], AX.X, ALU.max).then_inc(tested, 1)
            v.wait_ge(tested, 3)
            v.tensor_scalar(far[:], o_ps[0:1, 1, 0:NCOL], limit, None, ALU.is_gt).then_inc(tested, 1)

            def peak(g, q):
                v.wait_ge(om_ready[q % 4], (g // 4) * 16 + 16)
                v.tensor_reduce(most_g[:], om_sb[:, q % 4, 2 * KG:OM].rearrange("p (k g) -> p g k", g=GROUPS), AX.X, ALU.max)\
                    .then_inc(maxed, 1)

            def centre(g, q):
                v.wait_ge(maxed, g + 1)
                wait(v, approved, g - 3)
                v.tensor_tensor(mask[:, q % 4].rearrange("p (k g) -> p k g", g=GROUPS),
                                om_sb[:, q % 4, 2 * KG:OM].rearrange("p (k g) -> p k g", g=GROUPS), spread(most_g[:], TAPS),
                                ALU.subtract).then_inc(centred, 1)

            def sum_up(g, q):
                v.wait_ge(exped, g + 1)
                v.tensor_reduce(total[:], mask[:, q % 4].rearrange("p (k g) -> p g k", g=GROUPS), AX.X, ALU.add).then_inc(summed, 1)

            def invert(g, q):
                v.wait_ge(summed, g + 1)
                hold(v, passed)
                v.reciprocal(total[:], total[:]).then_inc(inverted, 1)

            def divide(g, q):
                v.wait_ge(inverted, g + 1)
                dst = mask[:, q % 4].rearrange("p (k g) -> p k g", g=GROUPS)
                v.tensor_tensor(dst, dst, spread(total[:], TAPS), ALU.mult).then_inc(masked, 1)

            def weigh(g, q):
                v.wait_ge(masked, g + 1)
                v.wait_ge(hatted, g + 1)
                wait(v, built, (g - 1) * BUILDS)
                v.tensor_tensor(hatm[:, q % 2], hat[:, q % 2, :, KG:2 * KG], spread(mask[:, q % 4], SH), ALU.mult)\
                    .then_inc(weighted, 1)

            def multiply(g, n, q, h, dx):
                p = g * SPAN + dx
                if dx == 0:
                    v.wait_ge(built, g * BUILDS + BUILDS)
                slot = (q + dx) % RING
                before = h * (WIDE // RING + (slot < WIDE % RING))
                v.wait_ge(v_ready[slot], ((n - h * CHUNKS) + (q + dx) // RING + 1 + before) * 32)
                wait(v, used, p - RING + 1)
                shape = [PIX, SPAN * GROUPS, GC]
                w = along(wt[:, q % 2, dx].rearrange("p y g -> p (y g)"), GC)
                v.tensor_tensor(prod[:, (q * SPAN + dx) % RING].rearrange("p (a c) -> p a c", c=GC),
                                v_sb[:, slot].rearrange("p (a c) -> p a c", c=GC), w, ALU.mult)\
                    .then_inc(multiplied if dx in FOLDED else made, 1)

            def fold(g, q, dx):
                v.wait_ge(multiplied, g * len(FOLDED) + FOLDED.index(dx) + 1)
                at = (q * SPAN + dx) % RING
                low, high = prod[:, at, 0:FOLD * C], prod[:, at, FOLD * C:2 * FOLD * C]
                v.tensor_tensor(low, low, high, ALU.add).then_inc(made, 1)

            def take(g, q):
                v.wait_ge(o_made, g + 1)
                v.tensor_tensor(tok[:, q % 4], o_ps[0:PIX, q % 2, 0:C], bo_bc[:], ALU.add).then_inc(o_taken, 1)

            def measure(g, q):
                v.wait_ge(o_taken, g + 1)
                v.bn_stats(stats[:, q % 2], tok[:, q % 4]).then_inc(statted, 1)

            def gather_up(g, q):
                v.wait_ge(statted, g + 1)
                hold(v, passed)
                v.bn_aggr(mv[:, q % 2], stats[:, q % 2]).then_inc(aggred, 1)

            def guard(g, q):
                v.wait_ge(aggred, g + 1)
                v.tensor_scalar(mv[:, q % 2, 1:2], mv[:, q % 2, 1:2], EPS, None, ALU.add).then_inc(var_ready, 1)

            def scale(g, q):
                v.wait_ge(rstd_ready, g + 1)
                v.scalar_tensor_tensor(out=tok[:, q % 4], in0=tok[:, q % 4], scalar=mv[:, q % 2, 0:1], in1=gain_bc[:],
                                       op0=ALU.subtract, op1=ALU.mult).then_inc(scaled, 1)

            def add_x(g, q):
                v.wait_ge(scaled, g + 1)
                if q % 4 == 0:
                    v.wait_ge(x_ready[q // 4], (g // COLS) * 16 + 16)
                v.scalar_tensor_tensor(out=res[:, q], in0=tok[:, q % 4], scalar=rstd[:, q % 2:q % 2 + 1], in1=res[:, q],
                                       op0=ALU.mult, op1=ALU.add).then_inc(added, 1)

            def finish(g, q):
                v.wait_ge(added, g + 1)
                v.tensor_tensor(res[:, q], res[:, q], bias_bc[:], ALU.add).then_inc(finished, 1)

            def body(n, h):
                for j in range(COLS):
                    g = n * COLS + j

                    def do(step, d):
                        at = near(n, j, d)
                        if at:
                            step(*at)

                    do(peak, 2)
                    multiply(g, n, j, h, 0)
                    do(centre, 2)
                    do(scale, -3)
                    multiply(g, n, j, h, 1)
                    do(add_x, -3)
                    fold(g, j, 1)
                    multiply(g, n, j, h, 2)
                    do(finish, -3)
                    do(sum_up, 2)
                    multiply(g, n, j, h, 3)
                    do(take, -2)
                    do(invert, 2)
                    fold(g, j, 3)
                    multiply(g, n, j, h, 4)
                    do(divide, 2)
                    do(measure, -2)
                    multiply(g, n, j, h, 5)
                    do(gather_up, -2)
                    do(weigh, 2)
                    fold(g, j, 5)
                    multiply(g, n, j, h, 6)
                    do(guard, -2)

            for g in range(2):
                for step in (peak, centre, sum_up, invert, divide, weigh):
                    step(g, g)
            walk(body)(v)
            for g in range(NCOL - 3, NCOL):
                q = g % COLS
                for step in (take, measure, gather_up, guard)[0 if g > NCOL - 3 else 4:]:
                    step(g, q)
                for step in (scale, add_x, finish):
                    step(g, q)

        @block.scalar
        def _(act):
            act.wait_ge(w_ready, 16 * WLOADS)
            act.wait_ge(consts, SH + 5)
            act.activation(yT[:, 0, 0, 0:1], wo_sb[:, 0, 0:1], ACT.Exp).then_inc(warm, 1)
            act.wait_ge(warm, 1)

            def weigh(g, q):
                act.wait_ge(om_ready[q % 4], (g // 4) * 16 + 16)
                wait(act, built, (g - 1) * BUILDS)
                for s in range(SH):
                    act.activation(hat[:, q % 2, s], om_sb[:, q % 4, 0:2 * KG], ACT.Abs, bias=shift[:, s:s + 1])\
                        .then_inc(distanced, 1)
                act.wait_ge(distanced, g * SH + SH)
                both = hat[:, q % 2].rearrange("p s o -> p (s o)")
                act.activation(both, both, ACT.Relu, bias=shift[:, SH:SH + 1], scale=-1.0).then_inc(hatted, 1)

            def clear(g, q):
                wait(act, made, (g - 1) * SPAN)
                dst = wt[:, q % 2].rearrange("p x y g -> p (x y g)")
                act.activation(dst, nil[:].to_broadcast([PIX, SPAN * SPAN * GROUPS]), ACT.Copy).then_inc(cleared, 1)

            def exp(g, q):
                act.wait_ge(centred, g + 1)
                act.activation(mask[:, q % 4], mask[:, q % 4], ACT.Exp).then_inc(exped, 1)

            def take(g, q):
                act.wait_ge(used, g * SPAN + SPAN)
                wait(act, o_made, g - 1)
                act.activation(yT[:, q % 2], y_ps[:, q % 2, :, 0:PIX], ACT.Copy).then_inc(y_taken, 1)

            def body(n, h):
                for j in range(COLS):
                    for step, d in ((clear, 1), (weigh, 2), (exp, 2), (take, -1)):
                        at = near(n, j, d)
                        if at:
                            step(*at)

            for g in range(2):
                weigh(g, g)
                exp(g, g)
            clear(0, 0)
            walk(body)(act)
            take(NCOL - 1, COLS - 1)

        @block.tensor
        def _(pe):
            pe.wait_ge(w_ready, 16 * WLOADS)
            pe.transpose(o_ps[0:NCOL, 0, 0:PIX], reach_sb[:], id_sb[0:PIX, 0:PIX]).then_inc(tested, 1)
            pe.wait_ge(tested, 2)
            pe.transpose(o_ps[0:1, 1, 0:NCOL], most[:], id_sb[0:NCOL, 0:NCOL]).then_inc(tested, 1)
            pe.wait_ge(tested, 4)

            def project(g, q):
                pe.wait_ge(y_taken, g + 1)
                wait(pe, o_taken, g - 1)
                for c in range(KC):
                    ins = pe.matmul(o_ps[0:PIX, q % 2, 0:C], yT[:, q % 2, c], wo_sb[:, c], start=(c == 0), stop=(c == KC - 1))
                ins.then_inc(o_made, 1)

            def body(n, h):
                for j in range(COLS):
                    g = n * COLS + j
                    pe.wait_ge(approved, g + 1)
                    wait(pe, y_taken, g - 1)
                    for dx in range(SPAN):
                        pe.wait_ge(made, g * SPAN + dx + 1)
                        for dy in range(SPAN):
                            if dx in FOLDED and FOLD <= dy < 2 * FOLD:
                                continue
                            for c in range(KC):
                                at = dy * C + c * P
                                ins = pe.matmul(y_ps[:, j % 2, c, 0:PIX], prod[:, (j * SPAN + dx) % RING, at:at + P],
                                                id_sb[0:PIX, 0:PIX], start=(dx == 0 and dy == 0),
                                                stop=(dx == SPAN - 1 and dy == SPAN - 1))
                        ins.then_inc(used, 1)
                        back = near(n, j, -1)
                        if dx == 1 and back:
                            project(*back)

            walk(body)(pe)
            project(NCOL - 1, COLS - 1)


ROWS = 112
SUB = 4
MT = ROWS * SUB
NT = TOK // MT


def mlp(nc, tag, x, out, w1, b1, w2, b2, ident, eps, ln_in=None, ln_out=None, windows=False):
    HC = w1.shape[1] // P
    split = ln_in is not None
    xv = x.rearrange("(n p t) c -> n p (t c)", p=ROWS, t=SUB)
    ov = out.rearrange("(n p t) c -> n p (t c)", p=ROWS, t=SUB)
    ACROSS, RUNS, PAIR = SIDE // 8, 16, 2 * 64
    STORES = ACROSS if windows else 1
    with ExitStack() as ctx:
        def sb(name, shape):
            return ctx.enter_context(nc.sbuf_tensor(f"{tag}_{name}", shape, F32))

        def ps(name, shape):
            return ctx.enter_context(nc.psum_tensor(f"{tag}_{name}", shape, F32))

        sems = []

        def sem(name):
            sems.append(nc.alloc_semaphore(f"{tag}_{name}"))
            return sems[-1]

        w1_sb = sb("w1", [P, KC, HC * P])
        w2_sb = sb("w2", [P, HC, C])
        id_sb = sb("id", [P, P])
        b1_sb = sb("b1", [P, HC])
        b2_bc = sb("b2", [ROWS, C])
        gin = sb("gin", [P, KC])
        bin_ = sb("bin", [P, KC])
        gout = sb("gout", [ROWS, C])
        bout = sb("bout", [ROWS, C])
        gam = sb("gam", [ROWS, C])
        half = sb("half", [ROWS, SUB])
        xt = sb("xt", [ROWS, 2, SUB, C])
        xn = sb("xn", [ROWS, SUB, C])
        xb = sb("xb", [ROWS, 2, SUB, C])
        yo = sb("yo", [ROWS, 2, SUB, C])
        stats = sb("stats", [ROWS, SUB, 6])
        mv = sb("mv", [ROWS, SUB, 2])
        rstd = sb("rstd", [ROWS, SUB])
        stats2 = sb("stats2", [ROWS, SUB, 6])
        mv2 = sb("mv2", [ROWS, SUB, 2])
        rstd2 = sb("rstd2", [ROWS, SUB])
        xT = sb("xT", [P, 2, KC, MT])
        hT = sb("hT", [P, HC, MT])
        if split:
            w1_low = sb("w1_low", [P, KC, HC * P])
            w2_low = sb("w2_low", [P, HC, C])
            x_low = sb("x_low", [P, 2, KC, MT])
            h_low = sb("h_low", [P, HC, MT])
            w1_high = sb("w1_high", [P, KC, HC * P])
            w2_high = sb("w2_high", [P, HC, C])
            x_high = sb("x_high", [P, 2, KC, MT])
            h_high = sb("h_high", [P, HC, MT])
        tp = ps("tp", [P, KC, BANK])
        hp = ps("hp", [P, 4, BANK])
        yp = ps("yp", [P, 2, BANK])

        w_ready = sem("w_ready")
        x_ready = [sem(f"x_ready{k}") for k in range(2)]
        stored = [sem(f"stored{k}") for k in range(2)]
        consts = sem("consts")
        var_ready = sem("var_ready")
        rstd_ready = sem("rstd_ready")
        xn_ready = sem("xn_ready")
        turned = sem("turned")
        xT_ready = sem("xT_ready")
        h_psum = sem("h_psum")
        h_ready = sem("h_ready")
        y_psum = sem("y_psum")
        y_taken = sem("y_taken")
        xb_ready = sem("xb_ready")
        dve = sem("dve")
        passed = sem("passed")
        dve_in = sem("dve_in")
        warm = sem("warm")
        w_cut = sem("w_cut")
        x_cut = sem("x_cut")
        x_split = sem("x_split")
        h_cut = sem("h_cut")
        h_split = sem("h_split")
        var2_ready = sem("var2_ready")
        rstd2_ready = sem("rstd2_ready")
        out_ready = sem("out_ready")
        WLOADS = 5 + (2 if ln_in else 0) + (3 if ln_out else 0)

        def more(n):
            return not (isinstance(n, int) and n + 1 >= NT)

        ctx.callback(close_phase, nc, sems)
        def ahead(n):
            return not (isinstance(n, int) and n + 2 >= NT)

        block = ctx.enter_context(nc.Block())

        def each_tile(body):
            def run(eng):
                for n in range(2):
                    body(n, n % 2, 0)
                with eng.Fori(1, NT // 2 - 1) as i:
                    for k in range(2):
                        body(i * 2 + k, k, i)
                for n in range(NT - 2, NT):
                    body(n, n % 2, n // 2)
            return run

        def next_tile(n, k, i):
            return n + 1, 1 - k, i + k

        def finished(eng, n):
            if ln_out:
                wait(eng, out_ready, n + 1)
            else:
                wait(eng, y_taken, n * SUB + SUB)

        @block.sync
        def _(sp):
            def load(n, k):
                src = xv[n]
                if windows:
                    first = (n // 2) * (ACROSS * PAIR * C) + (n % 2) * (PAIR // 2 * C)
                    src = bass.AP(x.tensor, first, [[PAIR * C, ACROSS], [SUB * C, RUNS], [1, SUB * C]])
                sp.dma_start(xt[:, k].rearrange("p t c -> p (t c)"), src).then_inc(x_ready[k], 16)

            load(0, 0)
            load(1, 1)
            for dst, src in ([(id_sb[:], ident), (w1_sb[:], w1.rearrange("(k p) n -> p k n", p=P)),
                              (w2_sb[:], w2.rearrange("(k p) n -> p k n", p=P)), (b2_bc[:], row_bc(b2, ROWS))]):
                sp.dma_start(dst, src).then_inc(w_ready, 16)
            with nc.allow_non_contiguous_dma(reason="bias columns"):
                sp.dma_start(b1_sb[:], cols(b1)).then_inc(w_ready, 16)
                if ln_in:
                    sp.dma_start(gin[:], cols(ln_in[0])).then_inc(w_ready, 16)
                    sp.dma_start(bin_[:], cols(ln_in[1])).then_inc(w_ready, 16)
            if ln_out:
                for dst, src in ((gout, ln_out[0]), (bout, ln_out[1]), (gam, ln_out[2])):
                    sp.dma_start(dst[:], row_bc(src, ROWS)).then_inc(w_ready, 16)

            def store(n, k, i):
                finished(sp, n)
                if not windows:
                    sp.dma_start(ov[n], yo[:, k].rearrange("p t c -> p (t c)")).then_inc(stored[k], 16)
                    return
                for w in range(ACROSS):
                    first = n * (MT * C) + w * (2 * SUB * C)
                    dst = bass.AP(out.tensor, first, [[SIDE * C, RUNS // 2], [SUB * C, 2], [1, SUB * C]])
                    sp.dma_start(dst, yo[w * RUNS:(w + 1) * RUNS, k].rearrange("p t c -> p (t c)")).then_inc(stored[k], 16)

            def body(n, k, i):
                if not (isinstance(n, int) and n + 2 >= NT):
                    wait(sp, xn_ready if ln_in else turned, n + 1)
                    wait(sp, xb_ready, n + 1)
                    load(n + 2, k)
                store(n, k, i)

            each_tile(body)(sp)
            for k in range(2):
                sp.wait_ge(stored[k], 16 * STORES * (NT // 2))

        @block.gpsimd
        def _(pool):
            nc.gpsimd.memset(half[:], -0.5).then_inc(consts, 1)
            pool.wait_ge(consts, 1)
            pool.wait_ge(w_ready, 16 * WLOADS)
            if ln_out:
                nc.gpsimd.tensor_tensor(gout[:], gout[:], gam[:], ALU.mult).then_inc(consts, 1)
                nc.gpsimd.tensor_tensor(bout[:], bout[:], gam[:], ALU.mult).then_inc(consts, 1)
                pool.wait_ge(consts, 3)

            def first(n, k, i):
                pool.wait_ge(x_ready[k], 16 * i + 16)
                finished(pool, n - 2)
                row = bout if ln_out else b2_bc
                nc.gpsimd.tensor_tensor(xb[:, k], xt[:, k], row[:].rearrange("p (o c) -> p o c", o=1).to_broadcast([ROWS, SUB, C]), ALU.add).then_inc(xb_ready, 1)

            def root(n):
                if ln_in:
                    pool.wait_ge(var_ready, n + 1)
                    nc.gpsimd.tensor_tensor(rstd[:], mv[:, :, 1], half[:], ALU.pow).then_inc(rstd_ready, 1)

            def second(n):
                if ln_out:
                    pool.wait_ge(var2_ready, n + 1)
                    nc.gpsimd.tensor_tensor(rstd2[:], mv2[:, :, 1], half[:], ALU.pow).then_inc(rstd2_ready, 1)

            def body(n, k, i):
                if more(n):
                    first(*next_tile(n, k, i))
                if ahead(n):
                    root(n + 2)
                second(n)

            root(0)
            first(0, 0, 0)
            root(1)
            each_tile(body)(pool)

        @block.vector
        def _(v):
            v.wait_ge(w_ready, 16 * WLOADS)
            if ln_out:
                v.wait_ge(consts, 3)

            if split:
                for high, w in ((w1_high, w1_sb), (w2_high, w2_sb)):
                    cut(v, high[:], w[:]).then_inc(w_cut, 1)
                v.wait_ge(w_cut, 2)
                for low, w, high in ((w1_low, w1_sb, w1_high), (w2_low, w2_sb, w2_high)):
                    rest(v, low[:], w[:], high[:]).then_inc(w_cut, 1)

            def split_x(n, k):
                if not split:
                    return
                v.wait_ge(xT_ready, n * KC + KC)
                wait(v, h_psum, (n - 1) * HC)
                cut(v, x_high[:, k], xT[:, k]).then_inc(x_cut, 1)
                v.wait_ge(x_cut, n + 1)
                rest(v, x_low[:, k], xT[:, k], x_high[:, k]).then_inc(x_split, 1)

            def split_h(n):
                if not split:
                    return
                wait(v, y_psum, n * SUB)
                for c in range(HC + 1):
                    if c < HC:
                        v.wait_ge(h_ready, n * HC + c + 1)
                        cut(v, h_high[:, c], hT[:, c]).then_inc(h_cut, 1)
                    if c:
                        v.wait_ge(h_cut, n * HC + c)
                        rest(v, h_low[:, c - 1], hT[:, c - 1], h_high[:, c - 1]).then_inc(h_split, 1)

            def measure(n, k, i):
                if not ln_in:
                    return
                v.wait_ge(x_ready[k], 16 * i + 16)
                base = n * 2
                for t in range(SUB):
                    ins = nc.vector.bn_stats(stats[:, t], xt[:, k, t])
                ins.then_inc(dve_in, 1)
                v.wait_ge(dve_in, base + 1)
                hold(v, passed)
                for t in range(SUB):
                    ins = nc.vector.bn_aggr(mv[:, t], stats[:, t])
                ins.then_inc(dve_in, 1)
                v.wait_ge(dve_in, base + 2)
                nc.vector.tensor_scalar(mv[:, :, 1], mv[:, :, 1], eps, None, ALU.add).then_inc(var_ready, 1)

            def first(n, k):
                if not ln_in:
                    return
                v.wait_ge(rstd_ready, n + 1)
                v.wait_ge(var_ready, n + 1)
                wait(v, turned, n)
                for t in range(SUB):
                    ins = nc.vector.tensor_scalar(xn[:, t], xt[:, k, t], mv[:, t, 0:1], rstd[:, t:t + 1],
                                                  ALU.subtract, ALU.mult)
                ins.then_inc(xn_ready, 1)

            def second(n, k, i, rows=range(SUB)):
                v.wait_ge(xb_ready, n + 1)
                wait(v, stored[k], i * 16 * STORES)
                for t in rows:
                    v.wait_ge(y_psum, n * SUB + t + 1)
                    nc.vector.tensor_tensor(yo[:, k, t], yp[0:ROWS, t % 2, 0:C], b2_bc[:] if ln_out else xb[:, k, t],
                                            ALU.add).then_inc(y_taken, 1)
                if not ln_out:
                    return
                v.wait_ge(y_taken, n * SUB + SUB)
                base = n * 4
                for t in range(SUB):
                    ins = nc.vector.bn_stats(stats2[:, t], yo[:, k, t])
                ins.then_inc(dve, 1)
                v.wait_ge(dve, base + 1)
                hold(v, passed)
                for t in range(SUB):
                    ins = nc.vector.bn_aggr(mv2[:, t], stats2[:, t])
                ins.then_inc(dve, 1)
                v.wait_ge(dve, base + 2)
                nc.vector.tensor_scalar(mv2[:, :, 1], mv2[:, :, 1], eps, None, ALU.add).then_inc(var2_ready, 1)
                v.wait_ge(rstd2_ready, n + 1)
                v.wait_ge(var2_ready, n + 1)
                for t in range(SUB):
                    ins = nc.vector.tensor_scalar(yo[:, k, t], yo[:, k, t], mv2[:, t, 0:1], rstd2[:, t:t + 1],
                                                  ALU.subtract, ALU.mult)
                ins.then_inc(dve, 1)
                v.wait_ge(dve, base + 3)
                nc.vector.tensor_tensor(yo[:, k], yo[:, k], gout[:].rearrange("p (o c) -> p o c", o=1).to_broadcast([ROWS, SUB, C]),
                                        ALU.mult).then_inc(dve, 1)
                v.wait_ge(dve, base + 4)
                nc.vector.tensor_tensor(yo[:, k], yo[:, k], xb[:, k], ALU.add).then_inc(out_ready, 1)

            def body(n, k, i):
                split_h(n)
                if more(n):
                    first(n + 1, 1 - k)
                if split:
                    second(n, k, i, range(0, 2))
                    if more(n):
                        split_x(n + 1, 1 - k)
                    if ahead(n):
                        measure(n + 2, k, i + 1)
                    second(n, k, i, range(2, SUB))
                else:
                    second(n, k, i)

            measure(0, 0, 0)
            first(0, 0)
            measure(1, 1, 0)
            split_x(0, 0)
            each_tile(body)(v)

        @block.scalar
        def _(act):
            act.wait_ge(w_ready, 16 * WLOADS)
            nc.scalar.activation(hT[:, 0, 0:1], b1_sb[:, 0:1], ACT.Gelu).then_inc(warm, 1)
            act.wait_ge(warm, 1)

            def first(n, k, i):
                act.wait_ge(turned, n + 1)
                wait(act, h_psum, (n - 1) * HC)
                for c in range(KC):
                    if ln_in:
                        nc.scalar.activation(xT[:, k, c], tp[:, c, 0:MT], ACT.Identity, bias=bin_[:, c:c + 1],
                                             scale=gin[:, c:c + 1]).then_inc(xT_ready, 1)
                    else:
                        nc.scalar.activation(xT[:, k, c], tp[:, c, 0:MT], ACT.Identity).then_inc(xT_ready, 1)

            def second(n, k, i):
                wait(act, y_psum, n * SUB)
                for c in range(HC):
                    act.wait_ge(h_psum, n * HC + c + 1)
                    nc.scalar.activation(hT[:, c], hp[:, (k * HC + c) % 4, 0:MT], ACT.Gelu, bias=b1_sb[:, c:c + 1]).then_inc(h_ready, 1)

            def body(n, k, i):
                second(n, k, i)
                if more(n):
                    first(*next_tile(n, k, i))

            first(0, 0, 0)
            each_tile(body)(act)

        @block.tensor
        def _(pe):
            pe.wait_ge(w_ready, 16 * WLOADS)

            def turn(n, k, i):
                if ln_in:
                    pe.wait_ge(xn_ready, n + 1)
                else:
                    pe.wait_ge(x_ready[k], 16 * i + 16)
                wait(pe, xT_ready, n * KC)
                for t in range(SUB):
                    for c in range(KC):
                        src = xn[:, t, c * P:(c + 1) * P] if ln_in else xt[:, k, t, c * P:(c + 1) * P]
                        ins = nc.tensor.transpose(tp[:, c, t * ROWS:(t + 1) * ROWS], src, id_sb[0:ROWS, 0:ROWS])
                ins.then_inc(turned, 1)

            def product(to, left, right, last, first):
                if split:
                    return split_product(pe, to, left, right, first, last)
                return pe.matmul(to, left, right, start=first, stop=last)

            def up(n, k):
                if split:
                    pe.wait_ge(x_split, n + 1)
                pe.wait_ge(xT_ready, n * KC + KC)
                for c in range(HC):
                    wait(pe, h_ready, n * HC + c - 3)
                    for kc in range(KC):
                        at = slice(c * P, (c + 1) * P)
                        if split:
                            left, right = (w1_high[:, kc, at], w1_low[:, kc, at]), (x_high[:, k, kc], x_low[:, k, kc])
                        else:
                            left, right = w1_sb[:, kc, at], xT[:, k, kc]
                        ins = product(hp[:, (k * HC + c) % 4, 0:MT], left, right, kc == KC - 1, kc == 0)
                    ins.then_inc(h_psum, 1)

            def down(n, k, rows=range(SUB)):
                if not split:
                    pe.wait_ge(h_ready, n * HC + HC)
                for t in rows:
                    wait(pe, y_taken, n * SUB + t - 1)
                    for c in range(HC):
                        if split and t == 0:
                            pe.wait_ge(h_split, n * HC + c + 1)
                        at = slice(t * ROWS, (t + 1) * ROWS)
                        if split:
                            left, right = (h_high[:, c, at], h_low[:, c, at]), (w2_high[:, c], w2_low[:, c])
                        else:
                            left, right = hT[:, c, at], w2_sb[:, c]
                        ins = product(yp[0:ROWS, t % 2, 0:C], left, right, c == HC - 1, c == 0)
                    ins.then_inc(y_psum, 1)

            if split:
                pe.wait_ge(w_cut, 4)
            turn(0, 0, 0)

            def body(n, k, i):
                up(n, k)
                if split:
                    down(n, k, range(0, 2))
                if more(n):
                    turn(*next_tile(n, k, i))
                down(n, k, range(2, SUB) if split else range(SUB))

            each_tile(body)(pe)


WS = 7
WTOK = WS * WS
STRIPS = TOK // (SIDE * WS)
SROWS = 98
SSUB = 4
STOK = SROWS * SSUB
NW = SIDE // WS
HEADS = 8
HD = C // HEADS
QH = P // HD
PAIR = 64 + WTOK
TABLE = 2 * WS - 1


def swin_attention(nc, x, out, w_qkv, b_qkv, rpb, w_proj, b_proj, gain, bias, masks, ident):
    scale = float(HD) ** -0.5
    xv = x.rearrange("(s t p) c -> s p t c", p=SROWS, t=SSUB)
    ov = out.rearrange("(s t p) c -> s p t c", p=SROWS, t=SSUB)
    with ExitStack() as ctx:
        def sb(name, shape):
            return ctx.enter_context(nc.sbuf_tensor(f"sw_{name}", shape, F32))

        def ps(name, shape):
            return ctx.enter_context(nc.psum_tensor(f"sw_{name}", shape, F32))

        sems = []

        def sem(name):
            sems.append(nc.alloc_semaphore(f"sw_{name}"))
            return sems[-1]

        wq_sb = sb("wq", [P, KC, 3 * C])
        wp_sb = sb("wp", [P, KC, C])
        id_sb = sb("id", [P, P])
        bq_sb = sb("bq", [P, 6])
        bqs_sb = sb("bqs", [P, 2])
        bp_bc = sb("bp", [SROWS, C])
        gin = sb("gin", [P, KC])
        bin_ = sb("bin", [P, KC])
        half = sb("half", [SROWS, SSUB])
        rows = sb("rows", [PAIR, (TABLE * (WS - 1) + 2 * WS - 1 - (WS - 1)) * HEADS])
        rel = sb("rel", [PAIR, HEADS, WTOK])
        mask = sb("mask", [PAIR, 2, 2, WTOK])
        table = sb("table", [PAIR, NW, 2, HEADS * WTOK])
        xt = sb("xt", [SROWS, 2, SSUB, C])
        xn = sb("xn", [SROWS, SSUB, C])
        xb = sb("xb", [SROWS, 2, SSUB, C])
        yo = sb("yo", [SROWS, 2, SSUB, C])
        stats = sb("stats", [SROWS, SSUB, 6])
        mv = sb("mv", [SROWS, SSUB, 2])
        rstd = sb("rstd", [SROWS, SSUB])
        xT = sb("xT", [P, KC, NW, WTOK])
        qT = sb("qT", [P, 2, KC, NW, WTOK])
        kB = sb("kB", [P, 2, KC, NW, QH, WTOK])
        vT = sb("vT", [P, KC, NW, WTOK])
        vw = sb("vw", [WTOK, 2, NW, C])
        sc = sb("sc", [PAIR, 2, HEADS, WTOK])
        mx = sb("mx", [PAIR, 2, HEADS])
        sm = sb("sm", [PAIR, 2, HEADS])
        pT = sb("pT", [WTOK, 2, HEADS, PAIR])
        oT = sb("oT", [P, 2, KC, WS, SIDE])
        s_ps = ps("s_ps", [P, 2, BANK])
        p_ps = ps("p_ps", [P, 2, BANK])
        g_ps = ps("g_ps", [P, 2, BANK])
        y_ps = ps("y_ps", [P, 2, BANK])

        w_ready = sem("w_ready")
        made = sem("made")
        zeroed = sem("zeroed")
        x_ready = [sem(f"x_ready{k}") for k in range(2)]
        stored = [sem(f"stored{k}") for k in range(2)]
        ln = sem("ln")
        passed = sem("passed")
        pe_passed = sem("pe_passed")
        var_ready = sem("var_ready")
        rstd_ready = sem("rstd_ready")
        xn_ready = sem("xn_ready")
        xb_ready = sem("xb_ready")
        turned = sem("turned")
        g_made = sem("g_made")
        g_taken = sem("g_taken")
        scored = sem("scored")
        soft = sem("soft")
        exped = sem("exped")
        p_turned = sem("p_turned")
        p_taken = sem("p_taken")
        o_made = sem("o_made")
        o_taken = sem("o_taken")
        y_made = sem("y_made")
        y_taken = sem("y_taken")
        WLOADS = 8 + 2 * WS
        TURN = 2
        QKV = 6
        VT = 4
        G = TURN + QKV + VT
        NP_ = NW // 2
        SOFT = 7
        ctx.callback(close_phase, nc, sems)
        block = ctx.enter_context(nc.Block())

        def more(n):
            return not (isinstance(n, int) and n + 1 >= STRIPS)

        def ahead(n):
            return not (isinstance(n, int) and n + 2 >= STRIPS)

        def whole(n):
            return not (isinstance(n, int) and n < 1)

        def prev_of(n, k, i):
            return n - 1, 1 - k, i - 1 + k

        @block.sync
        def _(sp):
            def load(n, k):
                sp.dma_start(xt[:, k], xv[n]).then_inc(x_ready[k], 16)

            def store(n, k):
                wait(sp, y_taken, n * SSUB + SSUB)
                sp.dma_start(ov[n], yo[:, k]).then_inc(stored[k], 16)

            for k in range(2):
                sp.sem_inc(stored[k], 1)
            load(0, 0)
            load(1, 1)
            for dst, src in ((id_sb[:], ident), (wq_sb[:], w_qkv.rearrange("(k p) n -> p k n", p=P)),
                             (wp_sb[:], w_proj.rearrange("(k p) n -> p k n", p=P)), (bp_bc[:], row_bc(b_proj, SROWS)),
                             (mask[:], masks)):
                sp.dma_start(dst, src).then_inc(w_ready, 16)
            with nc.allow_non_contiguous_dma(reason="bias columns"):
                for dst, src in ((bq_sb, b_qkv), (gin, gain), (bin_, bias)):
                    sp.dma_start(dst[:], cols(src)).then_inc(w_ready, 16)
            run = rows.shape[1]
            for base in (0, 64):
                for i in range(WS):
                    src = bass.AP(rpb.tensor, TABLE * i * HEADS, [[HEADS, WS], [1, run]])
                    sp.dma_start(rows[base + i * WS:base + i * WS + WS], src).then_inc(w_ready, 16)

            def body(n, k, i):
                if ahead(n):
                    wait(sp, xn_ready, n + 1)
                    wait(sp, xb_ready, n + 1)
                    load(n + 2, k)
                if whole(n):
                    store(n - 1, 1 - k)

            by_pairs(STRIPS, body)(sp)
            store(STRIPS - 1, 1)
            for k in range(2):
                sp.wait_ge(stored[k], 16 * (STRIPS // 2) + 1)

        @block.gpsimd
        def _(pool):
            nc.gpsimd.memset(kB[:], 0.0).then_inc(zeroed, 1)
            nc.gpsimd.memset(half[:], -0.5).then_inc(zeroed, 1)
            pool.wait_ge(zeroed, 2)
            pool.wait_ge(w_ready, 16 * WLOADS)

            def first(n):
                pool.wait_ge(var_ready, n + 1)
                nc.gpsimd.tensor_tensor(rstd[:], mv[:, :, 1], half[:], ALU.pow).then_inc(rstd_ready, 1)

            def rest(n, k, i):
                pool.wait_ge(x_ready[k], i * 16 + 16)
                wait(pool, y_taken, (n - 1) * SSUB)
                nc.gpsimd.tensor_tensor(xb[:, k], xt[:, k], spread(bp_bc[:], SSUB), ALU.add).then_inc(xb_ready, 1)

            def body(n, k, i):
                if ahead(n):
                    first(n + 2)
                if more(n):
                    rest(*next_of(n, k, i))

            for n in range(2):
                first(n)
            rest(0, 0, 0)
            by_pairs(STRIPS, body)(pool)

        @block.vector
        def _(v):
            v.memset(s_ps[:], 0.0).then_inc(made, 1)
            v.memset(rel[:], 0.0).then_inc(made, 1)
            v.wait_ge(w_ready, 16 * WLOADS)
            v.wait_ge(made, 2)
            run = rows.shape[1]
            top = (TABLE + 1) * (WS - 1)
            for base in (0, 64):
                src = bass.AP(rows[:].tensor, base * run + top * HEADS,
                              [[run, WTOK], [1, HEADS], [-TABLE * HEADS, WS], [-HEADS, WS]])
                v.tensor_copy(rel[base:base + WTOK].rearrange("p h (i j) -> p h i j", i=WS), src).then_inc(made, 1)
            v.wait_ge(made, 4)
            for wh in range(NW):
                for last in range(2):
                    v.tensor_tensor(table[:, wh, last].rearrange("p (h m) -> p h m", h=HEADS), rel[:],
                                    spread(mask[:, int(wh == NW - 1), last], HEADS), ALU.add).then_inc(made, 1)
            v.tensor_scalar(bqs_sb[:], bq_sb[:, 0:2], scale, None, ALU.mult).then_inc(made, 1)
            v.wait_ge(made, 4 + 2 * NW + 1)

            def ln_stats(n, k, i):
                v.wait_ge(x_ready[k], i * 16 + 16)
                for t in range(SSUB):
                    ins = v.bn_stats(stats[:, t], xt[:, k, t])
                ins.then_inc(ln, 1)
                v.wait_ge(ln, n * 2 + 1)
                hold(v, passed)
                for t in range(SSUB):
                    ins = v.bn_aggr(mv[:, t], stats[:, t])
                ins.then_inc(ln, 1)
                v.wait_ge(ln, n * 2 + 2)
                v.tensor_scalar(mv[:, :, 1], mv[:, :, 1], EPS, None, ALU.add).then_inc(var_ready, 1)

            def ln_apply(n, k):
                v.wait_ge(rstd_ready, n + 1)
                v.wait_ge(var_ready, n + 1)
                wait(v, turned, n)
                for t in range(SSUB):
                    ins = v.tensor_scalar(xn[:, t], xt[:, k, t], mv[:, t, 0:1], rstd[:, t:t + 1],
                                          ALU.subtract, ALU.mult)
                ins.then_inc(xn_ready, 1)

            def start(n, p):
                a, base = sc[:, p % 2], (n * NP_ + p) * SOFT
                v.wait_ge(scored, n * NP_ + p + 1)
                wait(v, p_turned, (n * NP_ + p - 1) * 2)
                tab = table[:, n % NW, int(p == NP_ - 1)]
                v.tensor_tensor(a.rearrange("p h m -> p (h m)"), s_ps[0:PAIR, p % 2, 0:HEADS * WTOK], tab, ALU.add)\
                    .then_inc(soft, 1)
                seen(n, p, 1)
                v.tensor_reduce(mx[:, p % 2], a, AX.X, ALU.max).then_inc(soft, 1)
                seen(n, p, 2)
                v.tensor_scalar(mx[:, p % 2], mx[:, p % 2], 0.0, None, ALU.max).then_inc(soft, 1)
                seen(n, p, 3)
                v.scalar_tensor_tensor(out=a, in0=a, scalar=0.0, in1=along(mx[:, p % 2], WTOK), op0=ALU.max,
                                       op1=ALU.subtract).then_inc(soft, 1)

            STEP = {}
            for what in ("s0", "s1", "e0", "s2", "e1", "s3", "e2", "e3"):
                for j in range(4 if what[0] == "s" else 3):
                    STEP[int(what[1]), j + 1 if what[0] == "s" else j + 5] = len(STEP) + 1

            def seen(n, p, j):
                v.wait_ge(soft, n * NP_ * SOFT + STEP[p, j])

            def end(n, p):
                a = sc[:, p % 2]
                v.wait_ge(exped, n * NP_ + p + 1)
                v.tensor_reduce(sm[:, p % 2], a, AX.X, ALU.add).then_inc(soft, 1)
                seen(n, p, 5)
                v.reciprocal(sm[:, p % 2], sm[:, p % 2]).then_inc(soft, 1)
                seen(n, p, 6)
                v.tensor_tensor(a, a, along(sm[:, p % 2], WTOK), ALU.mult).then_inc(soft, 1)

            def finish(n, k, i):
                wait(v, xb_ready, n + 1)
                v.wait_ge(stored[k], i * 16 + 1)
                for t in range(SSUB):
                    v.wait_ge(y_made, n * SSUB + t + 1)
                    v.tensor_tensor(yo[:, k, t], y_ps[0:SROWS, (t + 1) % 2, 0:C], xb[:, k, t], ALU.add).then_inc(y_taken, 1)

            def body(n, k, i):
                start(n, 0)
                start(n, 1)
                if whole(n):
                    finish(*prev_of(n, k, i))
                end(n, 0)
                if ahead(n):
                    ln_stats(n + 2, k, i + 1)
                start(n, 2)
                end(n, 1)
                if ahead(n):
                    ln_apply(n + 2, k)
                start(n, 3)
                end(n, 2)
                end(n, 3)

            for n in range(2):
                ln_stats(n, n, 0)
                ln_apply(n, n)
            by_pairs(STRIPS, body)(v)
            finish(STRIPS - 1, 1, STRIPS // 2 - 1)

        order = [(int(w[1]), j + (1 if w[0] == "s" else 5)) for w in ("s0", "s1", "e0", "s2", "e1", "s3", "e2", "e3")
                 for j in range(4 if w[0] == "s" else 3)]

        def soft_at(n, p, j):
            return n * NP_ * SOFT + order.index((p, j)) + 1

        @block.scalar
        def _(act):
            act.wait_ge(w_ready, 16 * WLOADS)
            act.wait_ge(zeroed, 2)
            act.wait_ge(made, 4 + 2 * NW + 1)

            def g_bank(n, j):
                act.wait_ge(g_made, n * G + j + 1)
                return g_ps[:, j % 2]

            def take_turned(n):
                for c in range(KC):
                    src = g_bank(n, c)[:, 0:STOK].rearrange("p (i x) -> p i x", i=WS)
                    far = src[:, :, SIDE - NW // 2:SIDE]
                    to = xT[:, c].rearrange("p w (i j) -> p i w j", i=WS)
                    last = xT[:, c, NW - 1].rearrange("p (i j) -> p i j", i=WS)
                    edge = SHIFT + (NW - 1) * WS
                    for dst, s in ((to[:, :, 0:NW - 1], src[:, :, SHIFT:edge].rearrange("p i (w j) -> p i w j", j=WS)),
                                   (last[:, :, 0:SIDE - edge], src[:, :, edge:SIDE]),
                                   (last[:, :, SIDE - edge:WS], src[:, :, 0:SHIFT])):
                        ins = act.activation(dst, s, ACT.Identity, bias=bin_[:, c:c + 1], scale=gin[:, c:c + 1])
                    ins.then_inc(g_taken, 1)

            def take_qkv(n, k, j):
                src = g_bank(n, TURN + j)[:, 0:STOK]
                c = j % 2
                if j < 2:
                    act.activation(qT[:, k, c].rearrange("p w n -> p (w n)"), src, ACT.Relu, bias=bqs_sb[:, j:j + 1],
                                   scale=scale).then_inc(g_taken, 1)
                elif j < 4:
                    for h in range(QH):
                        a, b = h * HD, h * HD + HD
                        ins = act.activation(kB[a:b, k, c, :, h], src[a:b].rearrange("p (w m) -> p w m", w=NW), ACT.Relu,
                                             bias=bq_sb[a:b, j:j + 1])
                    ins.then_inc(g_taken, 1)
                else:
                    act.activation(vT[:, c].rearrange("p w n -> p (w n)"), src, ACT.Relu, bias=bq_sb[:, j:j + 1])\
                        .then_inc(g_taken, 1)

            def take_v(n, k):
                for j in range(VT):
                    src = g_bank(n, TURN + QKV + j)[0:WTOK]
                    act.activation(vw[:, k, 2 * j:2 * j + 2].rearrange("p w c -> p (w c)"), src, ACT.Copy).then_inc(g_taken, 1)

            def exp(n, p):
                act.wait_ge(soft, soft_at(n, p, 4))
                a = sc[:, p % 2].rearrange("p h m -> p (h m)")
                act.activation(a, a, ACT.Exp).then_inc(exped, 1)

            def take_p(n, p):
                wait(act, o_made, n * NP_ + p - 1)
                for j in range(2):
                    act.wait_ge(p_turned, (n * NP_ + p) * 2 + j + 1)
                    act.activation(pT[:, p % 2, j * QH:j * QH + QH].rearrange("p h m -> p (h m)"),
                                   p_ps[0:WTOK, j, 0:QH * PAIR], ACT.Copy).then_inc(p_taken, 1)

            def take_o(n, k, p):
                act.wait_ge(o_made, n * NP_ + p + 1)
                if p == 0:
                    wait(act, y_made, (n - 1) * SSUB)
                for c in range(KC):
                    src = y_ps[:, 0, c * 2 * WTOK:(c + 1) * 2 * WTOK].rearrange("p (w i j) -> p w i j", w=2, i=WS)
                    x0 = 2 * p * WS + SHIFT
                    dst = oT[:, k, c]
                    if p < NP_ - 1:
                        moves = ((dst[:, :, x0:x0 + 2 * WS].rearrange("p i (w j) -> p w i j", w=2), src),)
                    else:
                        x1 = x0 + WS
                        moves = ((dst[:, :, x0:x1], src[:, 0]), (dst[:, :, x1:SIDE], src[:, 1, :, 0:SIDE - x1]),
                                 (dst[:, :, 0:SHIFT], src[:, 1, :, SIDE - x1:WS]))
                    for d, s in moves:
                        ins = act.activation(d, s, ACT.Relu)
                ins.then_inc(o_taken, 1)

            def body(n, k, i):
                m, q, _ = next_of(n, k, i)
                go = more(n)
                if go:
                    take_turned(m)
                take_p(n, 0)
                exp(n, 1)
                take_o(n, k, 0)
                if go:
                    take_qkv(m, q, 0)
                exp(n, 2)
                take_p(n, 1)
                if go:
                    take_qkv(m, q, 1)
                take_o(n, k, 1)
                if go:
                    take_qkv(m, q, 2)
                exp(n, 3)
                take_p(n, 2)
                if go:
                    take_qkv(m, q, 3)
                take_o(n, k, 2)
                if go:
                    take_qkv(m, q, 4)
                take_p(n, 3)
                if go:
                    take_qkv(m, q, 5)
                take_o(n, k, 3)
                if go:
                    take_v(m, q)
                    exp(m, 0)

            take_turned(0)
            for j in range(6):
                take_qkv(0, 0, j)
            take_v(0, 0)
            exp(0, 0)
            by_pairs(STRIPS, body)(act)

        @block.tensor
        def _(pe):
            pe.wait_ge(w_ready, 16 * WLOADS)
            pe.wait_ge(made, 2)

            def g_bank(n, j):
                wait(pe, g_taken, n * G + j - 1)
                return g_ps[:, j % 2]

            def turn(n):
                pe.wait_ge(xn_ready, n + 1)
                for c in range(KC):
                    bank = g_bank(n, c)
                    for t in range(SSUB):
                        ins = pe.transpose(bank[:, t * SROWS:(t + 1) * SROWS], xn[:, t, c * P:(c + 1) * P],
                                           id_sb[0:SROWS, 0:SROWS])
                    ins.then_inc(g_made, 1)
                pe.wait_ge(g_made, n * G + TURN)
                pe.sem_inc(turned, 1)

            def qkv(n, j):
                if j == 0:
                    pe.wait_ge(g_taken, n * G + TURN)
                bank = g_bank(n, TURN + j)
                for c in range(KC):
                    ins = pe.matmul(bank[:, 0:STOK], wq_sb[:, c, j * P:(j + 1) * P], xT[:, c].rearrange("p w n -> p (w n)"),
                                    start=(c == 0), stop=(c == KC - 1))
                ins.then_inc(g_made, 1)

            def turn_v(n):
                for j in range(VT):
                    bank = g_bank(n, TURN + QKV + j)
                    if j == 0:
                        pe.wait_ge(g_taken, n * G + TURN + QKV)
                    hold(pe, pe_passed)
                    for w in range(2):
                        for c in range(KC):
                            ins = pe.transpose(bank[0:WTOK, (w * KC + c) * P:(w * KC + c + 1) * P], vT[:, c, 2 * j + w],
                                               id_sb[:])
                    ins.then_inc(g_made, 1)

            def scores(n, k, p):
                wait(pe, g_taken, n * G + TURN + 4)
                if p < 2:
                    wait(pe, soft, soft_at(n - 1, p + 2, 1))
                else:
                    wait(pe, soft, soft_at(n, p - 2, 1))
                for w in range(2):
                    for c in range(KC):
                        ins = pe.matmul(s_ps[64 * w:64 * w + WTOK, p % 2, c * QH * WTOK:(c + 1) * QH * WTOK],
                                        qT[:, k, c, 2 * p + w], kB[:, k, c, 2 * p + w].rearrange("p h m -> p (h m)"),
                                        start=True, stop=True)
                ins.then_inc(scored, 1)

            def turn_p(n, p):
                pe.wait_ge(soft, soft_at(n, p, 7))
                for j in range(2):
                    wait(pe, p_taken, (n * NP_ + p - 1) * 2 + j + 1)
                    hold(pe, pe_passed)
                    for h in range(QH):
                        ins = pe.transpose(p_ps[0:WTOK, j, h * PAIR:(h + 1) * PAIR], sc[:, p % 2, j * QH + h],
                                           id_sb[0:PAIR, 0:PAIR])
                    ins.then_inc(p_turned, 1)

            def weigh(n, k, p):
                if p == 0:
                    pe.wait_ge(g_taken, n * G + G)
                    wait(pe, y_taken, n * SSUB)
                wait(pe, o_taken, n * NP_ + p)
                for j in range(2):
                    wait(pe, p_taken, (n * NP_ + p) * 2 + j + 1)
                    hold(pe, pe_passed)
                    for w in range(2):
                        for h in range(QH):
                            ins = pe.matmul(y_ps[h * HD:(h + 1) * HD, 0, (j * 2 + w) * WTOK:(j * 2 + w + 1) * WTOK],
                                            vw[:, k, 2 * p + w, (j * QH + h) * HD:(j * QH + h + 1) * HD],
                                            pT[:, p % 2, j * QH + h, 64 * w:64 * w + WTOK], start=True, stop=True)
                ins.then_inc(o_made, 1)

            def project(n, k):
                pe.wait_ge(o_taken, n * NP_ + NP_)
                for t in range(SSUB):
                    if t >= 2:
                        pe.wait_ge(y_taken, n * SSUB + t - 1)
                    for c in range(KC):
                        rows_ = oT[:, k, c].rearrange("p i x -> p (i x)")[:, t * SROWS:(t + 1) * SROWS]
                        ins = pe.matmul(y_ps[0:SROWS, (t + 1) % 2, 0:C], rows_, wp_sb[:, c], start=(c == 0), stop=(c == KC - 1))
                    ins.then_inc(y_made, 1)

            def body(n, k, i):
                m, q, _ = next_of(n, k, i)
                go = more(n)
                def next_qkv(j):
                    if go:
                        qkv(m, j)

                if go:
                    turn(m)
                turn_p(n, 0)
                scores(n, k, 2)
                weigh(n, k, 0)
                next_qkv(0)
                turn_p(n, 1)
                next_qkv(1)
                weigh(n, k, 1)
                scores(n, k, 3)
                next_qkv(2)
                turn_p(n, 2)
                next_qkv(3)
                weigh(n, k, 2)
                next_qkv(4)
                turn_p(n, 3)
                next_qkv(5)
                weigh(n, k, 3)
                if go:
                    scores(m, q, 0)
                    turn_v(m)
                    scores(m, q, 1)
                project(n, k)

            turn(0)
            for j in range(6):
                qkv(0, j)
            scores(0, 0, 0)
            turn_v(0)
            scores(0, 0, 1)
            by_pairs(STRIPS, body)(pe)


def swin_masks():
    def region(last):
        return np.repeat([0, 1], [WS - SHIFT, SHIFT]) if last else np.zeros(WS, int)

    m = np.zeros((PAIR, 2, 2, WTOK), np.float32)
    for w in range(2):
        for strip in range(2):
            for pair in range(2):
                at = (region(strip)[:, None] * 2 + region(pair and w)[None, :]).reshape(-1)
                m[64 * w:64 * w + WTOK, strip, pair] = np.where(at[:, None] != at[None, :], -1e9, 0.0)
    return m


KEPT = SIDE // 2 + 1
LAMBDA = 0.01


def fourier_mix(nc, x, nat, out, w1, b1, w2, b2, consts, ident):
    NB, BS = w1.shape[1], w1.shape[2]
    NCOL, NROW, HINV, WINV = consts
    F2 = 2 * KEPT
    PADK = 32
    LINE = 2 * SIDE
    GQ = C // 4
    YC = BANK // GQ
    CPB = 8
    with ExitStack() as ctx:
        def sb(name, shape):
            return ctx.enter_context(nc.sbuf_tensor(f"fo_{name}", shape, F32))

        sems = []

        def sem(name):
            sems.append(nc.alloc_semaphore(f"fo_{name}"))
            return sems[-1]

        id_sb = sb("id", [P, P])
        ncol = sb("ncol", [SIDE, F2])
        nrow = sb("nrow", [SIDE, 2, F2])
        hinv = sb("hinv", [P, LINE])
        winv = sb("winv", [P, 2, 2 * SIDE])
        wt = sb("wt", [P, 2, 3, KC, P])
        bias = sb("bias", [P, 2, 2, KC])
        xs = sb("xs", [SIDE, 2, SIDE, P])
        a_sb = sb("a", [2 * SIDE, 2 * SIDE * GQ + 256])
        spec = sb("spec", [P, KEPT, 2, KEPT])
        mid = sb("mid", [P, KEPT, 2, KEPT])
        o2 = sb("o2", [P, KEPT, 2, 2, PADK])
        q_sb = sb("q", [P, GQ, 4, PADK])
        t_sb = sb("t", [P, LINE, GQ])
        ring = ctx.enter_context(nc.psum_tensor("fo_ring", [P, 8, BANK], F32))
        a1 = a_sb[0:SIDE, 0:P * F2].rearrange("p (c f) -> p c f", f=F2)
        res = [a_sb[:, a * SIDE * GQ:(a + 1) * SIDE * GQ].rearrange("p (y c) -> p y c", c=GQ) for a in range(2)]

        w_zero = sem("w_zero")
        passed = sem("passed")
        w_ready = sem("w_ready")
        negated = sem("negated")
        zeroed = sem("zeroed")
        x_free = sem("x_free")
        x_ready = [sem(f"x_ready{k}") for k in range(2)]
        made = sem("made")
        by_act = sem("by_act")
        by_dve = sem("by_dve")
        pair_free = sem("pair_free")
        clipped = sem("clipped")
        shrunk = sem("shrunk")
        res_free = sem("res_free")
        res_ready = [sem(f"res_ready{a}") for a in range(2)]
        summed = sem("summed")
        stored = [sem(f"stored{a}") for a in range(2)]
        reordered = sem("reordered")

        N_COL, N_ROW, N_MLP, N_T, N_H, N_W = P // CPB, -(-KEPT // CPB), 4, -(-KEPT // 4), GQ // 4, 2 * SIDE // YC
        UNIT = N_COL + N_ROW + 2 * N_MLP
        HALF = 2 * UNIT + N_T
        LAST = N_H + N_W
        U = 2 * HALF + 2 * LAST
        WCUT = (0, 15, KEPT)
        WLOADS = 4 * NB + 4 + 5

        def unit_at(kc, s):
            return kc * HALF + s * UNIT

        def inv_at(s):
            return 2 * HALF + s * LAST

        def on_dve(u):
            last = u - 2 * HALF
            return u % 2 == 1 or (last >= 0 and last % LAST >= N_H)

        n_of = {False: [0], True: [0]}
        for u in range(U):
            for e in (False, True):
                n_of[e].append(n_of[e][-1] + int(on_dve(u) == e))

        def taken(eng, it, upto):
            for e, s in ((False, by_act), (True, by_dve)):
                if n_of[e][upto]:
                    eng.wait_ge(s, it * n_of[e][U] + n_of[e][upto])

        ctx.callback(close_phase, nc, sems)
        block = ctx.enter_context(nc.Block())

        def image(ap, b):
            return ap[bass.ds(b * (SIDE * SIDE), SIDE * SIDE), :].rearrange("(y x) c -> x y c", x=SIDE)

        @block.sync
        def _(sp):
            sp.sem_inc(x_free, 2)
            sp.sem_inc(res_free, 2)
            n = 0
            sp.wait_ge(w_zero, 1)
            for layer, w, b in ((0, w1, b1), (1, w2, b2)):
                for r in range(2):
                    for blk in range(NB):
                        kc, q = blk // (NB // KC), blk % (NB // KC)
                        a = q * BS
                        sp.dma_start(wt[a:a + BS, layer, r, kc, a:a + BS], w[r, blk]).then_inc(w_ready, 16)
                        n += 1
                with nc.allow_non_contiguous_dma(reason="bias columns"):
                    for r in range(2):
                        sp.dma_start(bias[:, layer, r], b[r].rearrange("(k q) o -> (q o) k", k=KC)).then_inc(w_ready, 16)
                        n += 1
            for dst, src in ((id_sb, ident), (ncol, NCOL), (nrow, NROW), (hinv, HINV), (winv, WINV)):
                sp.dma_start(dst[:], src).then_inc(w_ready, 16)
                n += 1
            assert n == WLOADS
            with sp.Fori(0, BATCH // 2) as it:
                for kc in range(KC):
                    for s in range(2):
                        sp.wait_ge(x_free, it * 4 + kc * 2 + s + 1)
                        sp.dma_start(xs[:, s], image(x, it * 2 + s)[:, :, kc * P:(kc + 1) * P]).then_inc(x_ready[s], 16)
                sp.wait_ge(made, it * U + unit_at(KC - 1, 1) + N_COL + N_ROW)
                for s in range(2):
                    for a in range(2):
                        if s == 1:
                            sp.wait_ge(stored[a], it * 64 + 32)
                        src = image(x, it * 2 + s)
                        for q in range(2):
                            c0 = (2 * a + q) * GQ
                            dst = res[a][q * SIDE:(q + 1) * SIDE]
                            sp.dma_start(dst[:, SHIFT:SIDE], src[:, 0:SIDE - SHIFT, c0:c0 + GQ]).then_inc(res_ready[a], 16)
                            sp.dma_start(dst[:, 0:SHIFT], src[:, SIDE - SHIFT:SIDE, c0:c0 + GQ]).then_inc(res_ready[a], 16)
                    for a in range(2):
                        sp.wait_ge(summed, it * 4 + s * 2 + a + 1)
                        dst = image(nat, it * 2 + s)
                        for q in range(2):
                            c0 = (2 * a + q) * GQ
                            sp.dma_start(dst[:, :, c0:c0 + GQ], res[a][q * SIDE:(q + 1) * SIDE]).then_inc(stored[a], 16)
                for a in range(2):
                    sp.wait_ge(stored[a], it * 64 + 64)
                sp.sem_inc(res_free, 2)
                for d in range(2 * SIDE // 16):
                    src = nat[bass.ds(it * (2 * SIDE * SIDE) + d * 16 * SIDE, 16 * SIDE), :]
                    dst = out[bass.ds(it * (2 * SIDE * SIDE) + d * 16 * SIDE, 16 * SIDE), :]
                    sp.dma_start(dst.rearrange("(w r j) c -> r w (j c)", w=7, r=16),
                                 src.rearrange("(r w j) c -> r w (j c)", w=7, r=16)).then_inc(reordered, 16)
            sp.wait_ge(reordered, 16 * 2 * 7)

        @block.gpsimd
        def _(pool):
            pool.memset(wt[:], 0.0).then_inc(w_zero, 1)
            pool.memset(o2[:], 0.0).then_inc(zeroed, 1)
            pool.memset(q_sb[:], 0.0).then_inc(zeroed, 1)
            pool.wait_ge(w_ready, 16 * WLOADS)
            for layer in range(2):
                pool.tensor_scalar(wt[:, layer, 2], wt[:, layer, 1], -1.0, None, ALU.mult).then_inc(negated, 1)

        def evacuate(eng, dve):
            mine = by_dve if dve else by_act

            def bank(it, u):
                eng.wait_ge(made, it * U + u + 1)
                return ring[:, u % 8]

            def copy(dst, src, bias_=None, relu=False):
                if dve:
                    if bias_ is None:
                        return eng.tensor_copy(dst, src)
                    if relu:
                        return eng.tensor_scalar(dst, src, bias_, 0.0, ALU.add, ALU.max)
                    return eng.tensor_scalar(dst, src, bias_, None, ALU.add)
                if bias_ is None:
                    return eng.activation(dst, src, ACT.Copy)
                return eng.activation(dst, src, ACT.Relu if relu else ACT.Identity, bias=bias_)

            eng.sem_inc(pair_free, 1)
            with eng.Fori(0, BATCH // 2) as it:
                eng.wait_ge(res_free, it * 2 + 2)
                for kc in range(KC):
                    for s in range(2):
                        u = unit_at(kc, s)
                        for j in range(N_COL):
                            if on_dve(u + j) == dve:
                                src = bank(it, u + j)[0:SIDE, 0:CPB * F2]
                                copy(a1[:, j * CPB:(j + 1) * CPB].rearrange("p c f -> p (c f)"), src).then_inc(mine, 1)
                        u += N_COL
                        if kc or s:
                            eng.wait_ge(shrunk, it * 4 + kc * 2 + s)
                        for j in range(N_ROW):
                            if on_dve(u + j) == dve:
                                w0, w1_ = j * CPB, min(KEPT, (j + 1) * CPB)
                                src = bank(it, u + j)[:, 0:(w1_ - w0) * F2]
                                copy(spec[:, w0:w1_].rearrange("p w r h -> p (w r h)"), src).then_inc(mine, 1)
                        u += N_ROW
                        for layer in range(2):
                            for j in range(N_MLP):
                                if on_dve(u + j) == dve:
                                    r, w0, w1_ = j // 2, WCUT[j % 2], WCUT[j % 2 + 1]
                                    src = bank(it, u + j)[:, 0:(w1_ - w0) * KEPT].rearrange("p (w h) -> p w h", h=KEPT)
                                    dst = o2[:, w0:w1_, s, r, 0:KEPT] if layer else mid[:, w0:w1_, r]
                                    copy(dst, src, bias[:, layer, r, kc:kc + 1], relu=not layer).then_inc(mine, 1)
                            u += N_MLP
                        if dve:
                            taken(eng, it, u)
                            n = it * 4 + kc * 2 + s
                            v = o2[:, :, s, :, 0:KEPT]
                            eng.tensor_scalar(spec[:], v, LAMBDA, -LAMBDA, ALU.min, ALU.max).then_inc(clipped, 1)
                            eng.wait_ge(clipped, n + 1)
                            eng.tensor_tensor(v, v, spec[:], ALU.subtract).then_inc(shrunk, 1)
                    u = kc * HALF + 2 * UNIT
                    for j in range(N_T):
                        if on_dve(u + j) == dve:
                            w0, w1_ = j * 4, min(KEPT, j * 4 + 4)
                            src = bank(it, u + j)[:, 0:(w1_ - w0) * P].rearrange("p (w q g) -> p w q g", q=2, g=GQ)
                            dst = q_sb[:, :, 2 * kc:2 * kc + 2, w0:w1_].rearrange("p g q w -> p w q g")
                            copy(dst, src).then_inc(mine, 1)
                for s in range(2):
                    u = inv_at(s)
                    for j in range(N_H):
                        if on_dve(u + j) == dve:
                            src = bank(it, u + j)[:, 0:4 * LINE].rearrange("p (g l) -> p g l", l=LINE)
                            copy(t_sb[:, :, 4 * j:4 * j + 4].rearrange("p l g -> p g l"), src).then_inc(mine, 1)
                    u += N_H
                    if dve:
                        for a in range(2):
                            eng.wait_ge(res_ready[a], it * 128 + s * 64 + 64)
                            for j in range(N_W // 2):
                                src = bank(it, u + a * (N_W // 2) + j)[0:2 * SIDE].rearrange("p (y c) -> p y c", c=GQ)
                                part = res[a][:, j * YC:(j + 1) * YC]
                                eng.tensor_tensor(part, part, src, ALU.add).then_inc(mine, 1)
                            taken(eng, it, u + (a + 1) * (N_W // 2))
                            eng.sem_inc(summed, 1)
                eng.sem_inc(pair_free, 1)

        @block.vector
        def _(v):
            v.wait_ge(w_ready, 16 * WLOADS)
            v.wait_ge(zeroed, 2)
            evacuate(v, True)

        @block.scalar
        def _(act):
            act.wait_ge(w_ready, 16 * WLOADS)
            act.wait_ge(zeroed, 2)
            evacuate(act, False)

        @block.tensor
        def _(pe):
            pe.wait_ge(w_ready, 16 * WLOADS)
            pe.wait_ge(negated, 2)
            pe.wait_ge(zeroed, 2)
            with pe.Fori(0, BATCH // 2) as it:
                pe.wait_ge(pair_free, it * 2 + 2)

                def bank(u):
                    if u >= 8:
                        e = on_dve(u - 8)
                        pe.wait_ge(by_dve if e else by_act, it * n_of[e][U] + n_of[e][u - 7])
                    return ring[:, u % 8]

                for kc in range(KC):
                    for s in range(2):
                        u = unit_at(kc, s)
                        pe.wait_ge(x_ready[s], it * 32 + kc * 16 + 16)
                        for j in range(N_COL):
                            to = bank(u + j)
                            hold(pe, passed)
                            for c in range(CPB):
                                ins = pe.matmul(to[0:SIDE, c * F2:(c + 1) * F2], xs[:, s, :, j * CPB + c], ncol[:],
                                                start=True, stop=True)
                            ins.then_inc(made, 1)
                        pe.wait_ge(made, it * U + u + N_COL)
                        pe.sem_inc(x_free, 1)
                        u += N_COL
                        taken(pe, it, u)
                        for j in range(N_ROW):
                            to = bank(u + j)
                            hold(pe, passed)
                            for w in range(j * CPB, min(KEPT, (j + 1) * CPB)):
                                for r in range(2):
                                    ins = pe.matmul(to[:, (w % CPB) * F2:(w % CPB + 1) * F2], a1[:, :, r * KEPT + w],
                                                    nrow[:, r], start=(r == 0), stop=(r == 1))
                            ins.then_inc(made, 1)
                        u += N_ROW
                        for layer in range(2):
                            taken(pe, it, u)
                            src = mid if layer else spec
                            for j in range(N_MLP):
                                r, w0, w1_ = j // 2, WCUT[j % 2], WCUT[j % 2 + 1]
                                to = bank(u + j)[:, 0:(w1_ - w0) * KEPT]
                                for m, (part, which) in enumerate(((0, 0), (1, 2)) if r == 0 else ((1, 0), (0, 1))):
                                    ins = pe.matmul(to, wt[:, layer, which, kc], src[:, w0:w1_, part], start=(m == 0),
                                                    stop=(m == 1))
                                ins.then_inc(made, 1)
                            u += N_MLP
                    u = kc * HALF + 2 * UNIT
                    pe.wait_ge(shrunk, it * 4 + kc * 2 + 2)
                    for j in range(N_T):
                        to = bank(u + j)
                        hold(pe, passed)
                        for w in range(j * 4, min(KEPT, j * 4 + 4)):
                            ins = pe.transpose(to[:, (w % 4) * P:(w % 4 + 1) * P], o2[:, w].rearrange("p s r h -> p (s r h)"),
                                               id_sb[:])
                        ins.then_inc(made, 1)
                taken(pe, it, 2 * HALF)
                for s in range(2):
                    u = inv_at(s)
                    half = slice(64 * s, 64 * s + 64)
                    quads = q_sb[half].rearrange("p g q w -> p g (q w)")
                    for j in range(N_H):
                        to = bank(u + j)
                        hold(pe, passed)
                        for g in range(4):
                            ins = pe.matmul(to[:, g * LINE:(g + 1) * LINE], quads[:, 4 * j + g], hinv[half], start=True,
                                            stop=True)
                        ins.then_inc(made, 1)
                    u += N_H
                    taken(pe, it, u)
                    for a in range(2):
                        rows = slice(64 * a, 64 * a + 64)
                        for j in range(N_W // 2):
                            to = bank(u + a * (N_W // 2) + j)[0:2 * SIDE]
                            hold(pe, passed)
                            for r in range(2):
                                line = r * SIDE + j * YC
                                ins = pe.matmul(to, winv[rows, r], t_sb[rows, line:line + YC].rearrange("p y c -> p (y c)"),
                                                start=(r == 0), stop=(r == 1))
                            ins.then_inc(made, 1)


def image_dft():
    k = np.arange(KEPT)
    a = 2 * np.pi * np.outer(np.arange(SIDE), k) / SIDE
    ncol = np.concatenate([np.cos(a), -np.sin(a)], 1) / SIDE
    h = np.arange(SIDE - KEPT, SIDE)
    y = (np.arange(SIDE) + SHIFT) % SIDE
    a = 2 * np.pi * np.outer(y, h) / SIDE
    co, si = np.cos(a), np.sin(a)
    nrow = np.stack([np.concatenate([co, -si], 1), np.concatenate([si, co], 1)], 1)
    a = 2 * np.pi * np.outer(h, np.arange(SIDE)) / SIDE
    hinv = np.zeros((2, 2, 32, 2, SIDE))
    hinv[:, 0, :KEPT, 0], hinv[:, 0, :KEPT, 1] = np.cos(a), np.sin(a)
    hinv[:, 1, :KEPT, 0], hinv[:, 1, :KEPT, 1] = -np.sin(a), np.cos(a)
    weight = np.full((KEPT, 1), 2.0)
    weight[[0, -1]] = 1.0
    a = 2 * np.pi * np.outer(k, np.arange(SIDE)) / SIDE
    winv = np.zeros((4, 32, 2, 2, SIDE))
    im = -weight * np.sin(a) / SIDE
    im[[0, -1]] = 0.0
    for q in range(4):
        winv[q, :KEPT, 0, q % 2], winv[q, :KEPT, 1, q % 2] = weight * np.cos(a) / SIDE, im
    f = np.float32
    return (ncol.astype(f), nrow.astype(f), hinv.reshape(P, 2 * SIDE).astype(f), winv.reshape(P, 2, 2 * SIDE).astype(f))


def spectral_attention(nc, x, out, w_qkv, b_qkv, rpb, w_proj, b_proj, gain, bias, dft, idft, ident):
    WS = 8
    WTOK = WS * WS
    FT = dft.shape[1] // 2
    PAIRS = TOK // P
    HEADS = 8
    HD = C // HEADS
    QH = P // HD
    TABLE = 2 * WS - 1
    ALL = P + 2 * FT
    RUN = (TABLE * (WS - 1) + WS) * HEADS
    scale = float(HD) ** -0.5
    xv = x.rearrange("(n p) c -> n p c", p=P)
    ov = out.rearrange("(n p) c -> n p c", p=P)
    with ExitStack() as ctx:
        def sb(name, shape):
            return ctx.enter_context(nc.sbuf_tensor(f"sp_{name}", shape, F32))

        def ps(name, shape):
            return ctx.enter_context(nc.psum_tensor(f"sp_{name}", shape, F32))

        sems = []

        def sem(name):
            sems.append(nc.alloc_semaphore(f"sp_{name}"))
            return sems[-1]

        wq_sb = sb("wq", [P, KC, 3 * C])
        wq_high = sb("wq_high", [P, KC, 3 * C])
        wq_low = sb("wq_low", [P, KC, 3 * C])
        x_high = sb("x_high", [P, KC, P + 2 * FT])
        x_low = sb("x_low", [P, KC, P + 2 * FT])
        wp_sb = sb("wp", [P, KC, C])
        id_sb = sb("id", [P, P])
        dft_sb = sb("dft", [P, 2 * FT])
        idft_sb = sb("idft", [FT, WTOK])
        bq_sb = sb("bq", [P, 6])
        bqs_sb = sb("bqs", [P, 2])
        bp_bc = sb("bp", [P, C])
        g_bc = sb("g", [P, C])
        b_bc = sb("b", [P, C])
        half = sb("half", [P, 1])
        rows = sb("rows", [P, RUN])
        rel = sb("rel", [P, HEADS, WTOK])
        xt = sb("xt", [P, 2, C])
        xn = sb("xn", [P, 2, C])
        xb = sb("xb", [P, 2, C])
        yo = sb("yo", [P, 2, C])
        stats = sb("stats", [P, 6])
        mv = sb("mv", [P, 2])
        rstd = sb("rstd", [P, 1])
        xT = sb("xT", [P, KC, ALL])
        qT = sb("qT", [P, 2, KC, ALL])
        kB = sb("kB", [P, 2, KC, QH, ALL])
        vT = sb("vT", [P, KC, ALL])
        vs = sb("vs", [WTOK, 2, 2, C])
        vf = sb("vf", [FT, 2, 2, C])
        sc = sb("sc", [P, HEADS, WTOK])
        sf = sb("sf", [FT, 2, HEADS, FT])
        mx = sb("mx", [P, 3, HEADS])
        sm = sb("sm", [P, 3, HEADS])
        pT = sb("pT", [WTOK, HEADS, P])
        gp = sb("gp", [FT, 2, HEADS, WTOK])
        oT = sb("oT", [P, KC, P])
        s_ps = ps("s_ps", [P, BANK])
        f_ps = ps("f_ps", [P, 2, BANK])
        p_ps = ps("p_ps", [P, 2, BANK])
        o_ps = ps("o_ps", [P, BANK])
        g_ps = ps("g_ps", [P, 2, BANK])

        w_ready = sem("w_ready")
        made = sem("made")
        zeroed = sem("zeroed")
        x_ready = [sem(f"x_ready{k}") for k in range(2)]
        stored = [sem(f"stored{k}") for k in range(2)]
        ln = sem("ln")
        cut_made = sem("cut_made")
        x_split = sem("x_split")
        passed = sem("passed")
        pe_passed = sem("pe_passed")
        var_ready = sem("var_ready")
        rstd_ready = sem("rstd_ready")
        centred = sem("centred")
        affine = sem("affine")
        xn_ready = sem("xn_ready")
        xb_ready = sem("xb_ready")
        g_made = sem("g_made")
        g_taken = sem("g_taken")
        scored = sem("scored")
        soft = sem("soft")
        exped = sem("exped")
        p_made = sem("p_made")
        p_taken = sem("p_taken")
        o_made = sem("o_made")
        o_taken = sem("o_taken")
        y_made = sem("y_made")
        y_taken = sem("y_taken")
        WLOADS = 9 + 2 * WS
        TURN, SPECTRA, QKV, VS, VF = 0, 1, 2, 8, 9
        G = 10
        SPACE, FREQ = 0, (1, 2)
        steps = [(job, j) for job, js in ((0, (1, 2, 3)), (1, (1, 2)), (0, (4, 5, 6)), (2, (1, 2)), (1, (4, 5, 6)),
                                          (2, (4, 5, 6))) for j in js]
        ctx.callback(close_phase, nc, sems)
        block = ctx.enter_context(nc.Block())

        def soft_at(n, job, j):
            return n * len(steps) + steps.index((job, j)) + 1

        def more(n):
            return not (isinstance(n, int) and n + 1 >= PAIRS)

        def ahead(n):
            return not (isinstance(n, int) and n + 2 >= PAIRS)

        def prev_of(n, k, i):
            return n - 1, 1 - k, i - 1 + k

        def whole(n):
            return not (isinstance(n, int) and n < 1)

        @block.sync
        def _(sp):
            def load(n, k):
                sp.dma_start(xt[:, k], xv[n]).then_inc(x_ready[k], 16)

            def store(n, k):
                wait(sp, y_taken, n + 1)
                sp.dma_start(ov[n], yo[:, k]).then_inc(stored[k], 16)

            for k in range(2):
                sp.sem_inc(stored[k], 1)
            load(0, 0)
            load(1, 1)
            for dst, src in ((id_sb[:], ident), (wq_sb[:], w_qkv.rearrange("(k p) n -> p k n", p=P)),
                             (wp_sb[:], w_proj.rearrange("(k p) n -> p k n", p=P)), (bp_bc[:], row_bc(b_proj, P)),
                             (g_bc[:], row_bc(gain, P)), (b_bc[:], row_bc(bias, P)), (dft_sb[:], dft),
                             (idft_sb[:], idft)):
                sp.dma_start(dst, src).then_inc(w_ready, 16)
            with nc.allow_non_contiguous_dma(reason="bias columns"):
                sp.dma_start(bq_sb[:], cols(b_qkv)).then_inc(w_ready, 16)
            for base in (0, WTOK):
                for i in range(WS):
                    src = bass.AP(rpb.tensor, TABLE * i * HEADS, [[HEADS, WS], [1, RUN]])
                    sp.dma_start(rows[base + i * WS:base + i * WS + WS], src).then_inc(w_ready, 16)

            def body(n, k, i):
                if not (isinstance(n, int) and n + 2 >= PAIRS):
                    wait(sp, centred, n + 1)
                    wait(sp, xb_ready, n + 1)
                    load(n + 2, k)
                if whole(n):
                    store(n - 1, 1 - k)

            by_pairs(PAIRS, body)(sp)
            store(PAIRS - 1, 1)
            for k in range(2):
                sp.wait_ge(stored[k], 16 * (PAIRS // 2) + 1)

        @block.gpsimd
        def _(pool):
            pool.memset(kB[:], 0.0).then_inc(zeroed, 1)
            pool.memset(half[:], -0.5).then_inc(zeroed, 1)
            pool.wait_ge(zeroed, 2)
            pool.wait_ge(w_ready, 16 * WLOADS)

            def first(n, k, i):
                pool.wait_ge(var_ready, n + 1)
                pool.tensor_tensor(rstd[:], mv[:, 1:2], half[:], ALU.pow).then_inc(rstd_ready, 1)
                pool.wait_ge(centred, n + 1)
                pool.tensor_tensor(xn[:, k], xn[:, k], g_bc[:], ALU.mult).then_inc(affine, 1)
                pool.wait_ge(affine, n + 1)
                pool.tensor_tensor(xn[:, k], xn[:, k], b_bc[:], ALU.add).then_inc(xn_ready, 1)

            def rest(n, k, i):
                pool.wait_ge(x_ready[k], i * 16 + 16)
                wait(pool, y_taken, n - 1)
                pool.tensor_tensor(xb[:, k], xt[:, k], bp_bc[:], ALU.add).then_inc(xb_ready, 1)

            def body(n, k, i):
                if ahead(n):
                    first(n + 2, k, i + 1)
                if more(n):
                    rest(*next_of(n, k, i))

            for n in range(2):
                first(n, n, 0)
            rest(0, 0, 0)
            by_pairs(PAIRS, body)(pool)

        @block.vector
        def _(v):
            v.wait_ge(w_ready, 16 * WLOADS)
            top = (TABLE + 1) * (WS - 1)
            src = bass.AP(rows[:].tensor, top * HEADS, [[RUN, P], [1, HEADS], [-TABLE * HEADS, WS], [-HEADS, WS]])
            v.tensor_copy(rel[:].rearrange("p h (i j) -> p h i j", i=WS), src).then_inc(made, 1)
            v.tensor_scalar(bqs_sb[:], bq_sb[:, 0:2], scale, None, ALU.mult).then_inc(made, 1)
            v.wait_ge(made, 2)
            cut(v, wq_high[:], wq_sb[:]).then_inc(cut_made, 1)
            v.wait_ge(cut_made, 1)
            rest(v, wq_low[:], wq_sb[:], wq_high[:]).then_inc(x_split, 1)

            def split_x(n):
                v.wait_ge(g_taken, n * G + SPECTRA + 1)
                wait(v, g_made, (n - 1) * G + VS)
                cut(v, x_high[:], xT[:]).then_inc(cut_made, 1)
                v.wait_ge(cut_made, n + 2)
                rest(v, x_low[:], xT[:], x_high[:]).then_inc(x_split, 1)

            def ln_stats(n, k, i):
                v.wait_ge(x_ready[k], i * 16 + 16)
                v.bn_stats(stats[:], xt[:, k]).then_inc(ln, 1)
                v.wait_ge(ln, n * 2 + 1)
                hold(v, passed)
                v.bn_aggr(mv[:], stats[:]).then_inc(ln, 1)
                v.wait_ge(ln, n * 2 + 2)
                v.tensor_scalar(mv[:, 1:2], mv[:, 1:2], EPS, None, ALU.add).then_inc(var_ready, 1)

            def ln_apply(n, k):
                v.wait_ge(rstd_ready, n + 1)
                v.wait_ge(var_ready, n + 1)
                wait(v, g_made, (n - 2) * G + SPECTRA + 1)
                v.tensor_scalar(xn[:, k], xt[:, k], mv[:, 0:1], rstd[:], ALU.subtract, ALU.mult).then_inc(centred, 1)

            def views(job):
                if job == SPACE:
                    return sc[:], mx[:, 0], sm[:, 0], WTOK
                return sf[:, job - 1], mx[0:FT, job], sm[0:FT, job], FT

            def seen(n, job, j):
                v.wait_ge(soft, soft_at(n, job, j))

            def start(n, job):
                a, m, _, size = views(job)
                v.wait_ge(scored, n * 3 + job + 1)
                if job == SPACE:
                    wait(v, p_made, (n - 1) * 4 + 2)
                    v.tensor_tensor(a.rearrange("p h m -> p (h m)"), s_ps[:], rel[:].rearrange("p h m -> p (h m)"),
                                    ALU.add).then_inc(soft, 1)
                    seen(n, job, 1)
                    v.tensor_reduce(m, a, AX.X, ALU.max).then_inc(soft, 1)
                    seen(n, job, 2)
                    v.tensor_tensor(a, a, along(m, size), ALU.subtract).then_inc(soft, 1)
                else:
                    raw = f_ps[0:FT, :, 0:QH * FT].rearrange("p c (h m) -> p c h m", h=QH)
                    wait(v, p_made, (n - 1) * 4 + 2 + job)
                    v.tensor_reduce(m.rearrange("p (c h) -> p c h", c=2), raw, AX.X, ALU.max).then_inc(soft, 1)
                    seen(n, job, 1)
                    for c in range(2):
                        ins = v.tensor_tensor(a[:, c * QH:c * QH + QH], raw[:, c], along(m[:, c * QH:c * QH + QH], size),
                                              ALU.subtract)
                    ins.then_inc(soft, 1)

            def end(n, job):
                a, _, s, size = views(job)
                v.wait_ge(exped, n * 3 + job + 1)
                v.tensor_reduce(s, a, AX.X, ALU.add).then_inc(soft, 1)
                seen(n, job, 4)
                v.reciprocal(s, s).then_inc(soft, 1)
                seen(n, job, 5)
                v.tensor_tensor(a, a, along(s, size), ALU.mult).then_inc(soft, 1)

            def finish(n, k, i):
                v.wait_ge(xb_ready, n + 1)
                v.wait_ge(stored[k], i * 16 + 1)
                v.wait_ge(y_made, n + 1)
                v.tensor_tensor(yo[:, k], o_ps[:, C:2 * C], xb[:, k], ALU.add).then_inc(y_taken, 1)

            def body(n, k, i):
                start(n, SPACE)
                start(n, FREQ[0])
                if more(n):
                    split_x(n + 1)
                if whole(n):
                    finish(*prev_of(n, k, i))
                if ahead(n):
                    ln_stats(n + 2, k, i + 1)
                end(n, SPACE)
                if ahead(n):
                    ln_apply(n + 2, k)
                start(n, FREQ[1])
                end(n, FREQ[0])
                end(n, FREQ[1])

            for n in range(2):
                ln_stats(n, n, 0)
                ln_apply(n, n)
            split_x(0)
            by_pairs(PAIRS, body)(v)
            finish(PAIRS - 1, 1, PAIRS // 2 - 1)

        @block.scalar
        def _(act):
            act.wait_ge(w_ready, 16 * WLOADS)
            act.wait_ge(zeroed, 2)
            act.wait_ge(made, 2)

            def g_bank(n, j):
                act.wait_ge(g_made, n * G + j + 1)
                return g_ps[:, j % 2]

            def take_turned(n):
                src = g_bank(n, TURN)[:, 0:KC * P].rearrange("p (c t) -> p c t", c=KC)
                act.activation(xT[:, :, 0:P], src, ACT.Copy).then_inc(g_taken, 1)
                src = g_bank(n, SPECTRA)[:, 0:KC * 2 * FT].rearrange("p (c t) -> p c t", c=KC)
                act.activation(xT[:, :, P:ALL], src, ACT.Copy).then_inc(g_taken, 1)

            def take_qkv(n, k, j):
                src = g_bank(n, QKV + j)[:, 0:ALL]
                c = j % 2
                if j < 2:
                    act.activation(qT[:, k, c], src, ACT.Identity, bias=bqs_sb[:, j:j + 1], scale=scale).then_inc(g_taken, 1)
                elif j < 4:
                    for h in range(QH):
                        a, b = h * HD, h * HD + HD
                        ins = act.activation(kB[a:b, k, c, h], src[a:b], ACT.Identity, bias=bq_sb[a:b, j:j + 1])
                    ins.then_inc(g_taken, 1)
                else:
                    act.activation(vT[:, c], src, ACT.Identity, bias=bq_sb[:, j:j + 1]).then_inc(g_taken, 1)

            def take_v(n, k):
                for j, dst, size in ((VS, vs, WTOK), (VF, vf, FT)):
                    src = g_bank(n, j)[0:size]
                    act.activation(dst[:, k].rearrange("p w c -> p (w c)"), src, ACT.Copy).then_inc(g_taken, 1)

            def exp(n, job):
                act.wait_ge(soft, soft_at(n, job, 3 if job == SPACE else 2))
                a = (sc[:] if job == SPACE else sf[:, job - 1]).rearrange("p h m -> p (h m)")
                act.activation(a, a, ACT.Exp).then_inc(exped, 1)

            def take_p(n, j):
                act.wait_ge(p_made, n * 4 + j + 1)
                if j < 2:
                    dst, src = pT[:, j * QH:j * QH + QH].rearrange("p h m -> p (h m)"), p_ps[0:WTOK, j % 2]
                else:
                    dst, src = gp[:, j - 2].rearrange("p h m -> p (h m)"), p_ps[0:FT, j % 2]
                act.activation(dst, src, ACT.Copy).then_inc(p_taken, 1)

            def take_o(n):
                act.wait_ge(o_made, n + 1)
                wait(act, y_made, n)
                act.activation(oT[:].rearrange("p c t -> p (c t)"), o_ps[:, 0:C], ACT.Copy).then_inc(o_taken, 1)

            def body(n, k, i):
                m, q, _ = next_of(n, k, i)
                go = more(n)
                exp(n, FREQ[0])
                if go:
                    for j in range(3):
                        take_qkv(m, q, j)
                wait(act, o_made, n)
                take_p(n, 0)
                take_p(n, 1)
                exp(n, FREQ[1])
                if go:
                    for j in range(3, 5):
                        take_qkv(m, q, j)
                take_p(n, 2)
                if go:
                    take_qkv(m, q, 5)
                take_p(n, 3)
                if go:
                    take_v(m, q)
                    exp(m, SPACE)
                if ahead(n):
                    take_turned(n + 2)
                take_o(n)

            take_turned(0)
            for j in range(6):
                take_qkv(0, 0, j)
            take_v(0, 0)
            exp(0, SPACE)
            take_turned(1)
            by_pairs(PAIRS, body)(act)

        @block.tensor
        def _(pe):
            pe.wait_ge(w_ready, 16 * WLOADS)

            def g_bank(n, j):
                wait(pe, g_taken, n * G + j - 1)
                return g_ps[:, j % 2]

            def turn(n, k):
                pe.wait_ge(xn_ready, n + 1)
                bank = g_bank(n, TURN)
                for c in range(KC):
                    ins = pe.transpose(bank[:, c * P:(c + 1) * P], xn[:, k, c * P:(c + 1) * P], id_sb[:])
                ins.then_inc(g_made, 1)
                bank = g_bank(n, SPECTRA)
                for c in range(KC):
                    ins = pe.matmul(bank[:, c * 2 * FT:(c + 1) * 2 * FT], xn[:, k, c * P:(c + 1) * P], dft_sb[:],
                                    start=True, stop=True)
                ins.then_inc(g_made, 1)

            def qkv(n, j):
                if j == 0:
                    pe.wait_ge(x_split, n + 2)
                bank = g_bank(n, QKV + j)
                for c in range(KC):
                    ins = split_product(pe, bank[:, 0:ALL], (wq_high[:, c, j * P:(j + 1) * P], wq_low[:, c, j * P:(j + 1) * P]),
                                        (x_high[:, c], x_low[:, c]), c == 0, c == KC - 1)
                ins.then_inc(g_made, 1)

            def turn_v(n):
                pe.wait_ge(g_taken, n * G + VS)
                for j, size, at in ((VS, WTOK, 0), (VF, FT, P)):
                    bank = g_bank(n, j)
                    hold(pe, pe_passed)
                    for w in range(2):
                        for c in range(KC):
                            ins = pe.transpose(bank[0:size, (w * KC + c) * P:(w * KC + c + 1) * P],
                                               vT[:, c, at + w * size:at + (w + 1) * size], id_sb[:])
                    ins.then_inc(g_made, 1)

            def scores(n, k, job):
                if job == SPACE:
                    pe.wait_ge(g_taken, n * G + QKV + 4)
                    wait(pe, soft, soft_at(n - 1, SPACE, 1))
                    hold(pe, pe_passed)
                    for w in range(2):
                        for c in range(KC):
                            a = w * WTOK
                            ins = pe.matmul(s_ps[a:a + WTOK, c * QH * WTOK:(c + 1) * QH * WTOK], qT[:, k, c, a:a + WTOK],
                                            kB[:, k, c, :, a:a + WTOK], start=True, stop=True)
                else:
                    wait(pe, soft, soft_at(n, 1, 2) if job == 2 else soft_at(n - 1, 2, 2))
                    for c in range(KC):
                        a = P + (job - 1) * FT
                        ins = pe.matmul(f_ps[0:FT, c, 0:QH * FT], qT[:, k, c, a:a + FT], kB[:, k, c, :, a:a + FT],
                                        start=True, stop=True)
                ins.then_inc(scored, 1)

            def turn_p(n):
                pe.wait_ge(soft, soft_at(n, SPACE, 6))
                for j in range(2):
                    wait(pe, p_taken, n * 4 + j - 1)
                    hold(pe, pe_passed)
                    for h in range(QH):
                        ins = pe.transpose(p_ps[0:WTOK, j, h * P:(h + 1) * P], sc[:, j * QH + h], id_sb[:])
                    ins.then_inc(p_made, 1)

            def back(n, w):
                pe.wait_ge(soft, soft_at(n, FREQ[w], 6))
                wait(pe, p_taken, n * 4 + w + 1)
                for h in range(HEADS):
                    ins = pe.matmul(p_ps[0:FT, w, h * WTOK:(h + 1) * WTOK], sf[:, w, h], idft_sb[:], start=True, stop=True)
                ins.then_inc(p_made, 1)

            def weigh(n, k):
                pe.wait_ge(p_taken, n * 4 + 4)
                pe.wait_ge(g_taken, n * G + G)
                wait(pe, y_taken, n)
                hold(pe, pe_passed)
                for h in range(HEADS):
                    c, q = h // QH, h % QH
                    for w in range(2):
                        a = c * P + w * WTOK
                        to = o_ps[q * HD:(q + 1) * HD, a:a + WTOK]
                        pe.matmul(to, vs[:, k, w, h * HD:(h + 1) * HD], pT[:, h, w * WTOK:(w + 1) * WTOK], start=True,
                                  stop=False)
                        ins = pe.matmul(to, vf[:, k, w, h * HD:(h + 1) * HD], gp[:, w, h], start=False, stop=True)
                ins.then_inc(o_made, 1)

            def project(n):
                pe.wait_ge(o_taken, n + 1)
                for c in range(KC):
                    ins = pe.matmul(o_ps[:, C:2 * C], oT[:, c], wp_sb[:, c], start=(c == 0), stop=(c == KC - 1))
                ins.then_inc(y_made, 1)

            def body(n, k, i):
                m, q, _ = next_of(n, k, i)
                go = more(n)
                if whole(n):
                    project(n - 1)
                if go:
                    qkv(m, 0)
                scores(n, k, FREQ[1])
                if go:
                    for j in range(1, 3):
                        qkv(m, j)
                turn_p(n)
                if go:
                    for j in range(3, 5):
                        qkv(m, j)
                back(n, 0)
                if go:
                    qkv(m, 5)
                    scores(m, q, SPACE)
                back(n, 1)
                if go:
                    turn_v(m)
                    scores(m, q, FREQ[0])
                if ahead(n):
                    turn(n + 2, k)
                weigh(n, k)

            turn(0, 0)
            for j in range(6):
                qkv(0, j)
            scores(0, 0, SPACE)
            turn_v(0)
            scores(0, 0, FREQ[0])
            turn(1, 1)
            by_pairs(PAIRS, body)(pe)
            project(PAIRS - 1)


def window_dft(n=64):
    half = n // 2 + 1
    a = 2 * np.pi * np.outer(np.arange(n), np.arange(half)) / n
    fwd = np.concatenate([np.cos(a), -np.sin(a)], 1) / np.sqrt(n)
    weight = np.full(half, 2.0)
    weight[[0, -1]] = 1.0
    re, im = np.cos(a) * weight, -np.sin(a) * weight
    im[:, [0, -1]] = 0.0
    inv = (np.concatenate([re, im], 1) / np.sqrt(n)).T
    twice = np.zeros((2 * n, 4 * half))
    twice[:n, :2 * half] = fwd
    twice[n:, 2 * half:] = fwd
    return twice.astype(np.float32), inv.astype(np.float32)


def network(nc: bass.Bass, a, out):
    def scratch(name, shape):
        return nc.dram_tensor(name, shape, F32, kind="Internal").ap()

    ident = a["ident"]
    x = a["x"]
    xp = scratch("xp", [2 * WIDE * 2 * WIDE, C])
    om = scratch("om", [NCOL * PIX, OM])
    reach = scratch("reach", [PIX, NCOL])
    one, two, three = (scratch(name, [TOK, C]) for name in ("one", "two", "three"))
    l0 = {k[3:]: v for k, v in a.items() if k.startswith("L0_")}
    l1 = {k[3:]: v for k, v in a.items() if k.startswith("L1_")}
    l2 = {k[3:]: v for k, v in a.items() if k.startswith("L2_")}
    l3 = {k[3:]: v for k, v in a.items() if k.startswith("L3_")}

    dcn_front(nc, x, xp, om, reach, l0["w_in"], l0["b_in"], l0["w_dw"], l0["b_dw"], l0["ln_dw_g"], l0["ln_dw_b"], l0["w_om"],
              l0["b_om"], ident)
    dcn_sample(nc, xp, om, reach, x, one, l0["w_out"], l0["b_out"], l0["ln1_g"], l0["ln1_b"], l0["gamma1"], ident, a["places"])
    mlp(nc, "m0", one, two, l0["w_fc1"], l0["b_fc1"], l0["w_fc2"], l0["b_fc2"], ident, EPS,
        ln_out=(l0["ln2_g"], l0["ln2_b"], l0["gamma2"]))
    swin_attention(nc, two, one, l1["w_qkv"], l1["b_qkv"], l1["rpb"], l1["w_proj"], l1["b_proj"], l1["gamma1"], l1["beta1"],
                   a["masks"], ident)
    mlp(nc, "m1", one, two, l1["w_fc1"], l1["b_fc1"], l1["w_fc2"], l1["b_fc2"], ident, EPS, ln_in=(l1["gamma2"], l1["beta2"]))
    fourier_mix(nc, two, three, one, l2["w1"], l2["b1"], l2["w2"], l2["b2"], [a[f"image_dft{i}"] for i in range(4)], ident)
    spectral_attention(nc, one, two, l3["qkv_w"], l3["qkv_b"], l3["rpb_table"], l3["proj_w"], l3["proj_b"], l3["norm1_w"],
                       l3["norm1_b"], a["window_dft"], a["window_idft"], ident)
    mlp(nc, "m3", two, out, l3["fc1_w"], l3["fc1_b"], l3["fc2_w"], l3["fc2_b"], ident, EPS,
        ln_in=(l3["norm2_w"], l3["norm2_b"]), windows=True)


def kernel(**inputs):
    import concourse.bacc as bacc
    from concourse.bass_utils import run_bass_kernel_spmd

    given = {k.replace("_conv_", "_"): np.asarray(v) for k, v in inputs.items()}
    w_off = given.pop("L0_w_off").reshape(C, GROUPS, TAPS, 2).transpose(0, 3, 2, 1).reshape(C, 2 * KG)
    w_mask = given.pop("L0_w_mask").reshape(C, GROUPS, TAPS).transpose(0, 2, 1).reshape(C, KG)
    b_off = given.pop("L0_b_off").reshape(GROUPS, TAPS, 2).transpose(2, 1, 0).reshape(-1)
    b_mask = given.pop("L0_b_mask").reshape(GROUPS, TAPS).transpose(1, 0).reshape(-1)
    given["L0_w_om"] = np.concatenate([w_off, w_mask], 1)
    given["L0_b_om"] = np.concatenate([b_off, b_mask])
    given["L0_w_dw"] = given["L0_w_dw"].reshape(TAPS, C).T
    given["x"] = given["x"].reshape(TOK, C)
    given.pop("L3_mask_matrix")
    for name in ("qkv_w", "proj_w", "fc1_w", "fc2_w"):
        given["L3_" + name] = given["L3_" + name].T
    given["ident"] = np.eye(P, dtype=np.float32)
    given["places"] = places()
    given["masks"] = swin_masks()
    given["window_dft"], given["window_idft"] = window_dft()
    for i, m in enumerate(image_dft()):
        given[f"image_dft{i}"] = m

    nc = bacc.Bacc("TRN2", target_bir_lowering=False, num_devices=1)
    arrays, args = {}, {}
    for name, value in given.items():
        value = np.ascontiguousarray(value)
        arrays[f"in_{name}"] = value
        args[name] = nc.dram_tensor(f"in_{name}", value.shape, mybir.dt.from_np(value.dtype), kind="ExternalInput").ap()
    out = nc.dram_tensor("out", (TOK, C), F32, kind="ExternalOutput").ap()
    network(nc, args, out)
    r = run_bass_kernel_spmd(nc, [arrays], core_ids=[0])
    return r.results[0]["out"].reshape(BATCH, SIDE, SIDE, C)
```
